# Optimizing a Trainium2 kernel written in Bass

```python
import numpy as np
import jax
import jax.numpy as jnp

def _softmax(x, axis=-1):
    return jax.nn.softmax(x, axis=axis)

def _gelu(x):
    return jax.nn.gelu(x, approximate=True)

def _silu(x):
    return jax.nn.silu(x)

def _sigmoid(x):
    return jax.nn.sigmoid(x)

def _layernorm(x, axis=-1, eps=1e-05):
    m = jnp.mean(x, axis=axis, keepdims=True)
    v = jnp.var(x, axis=axis, keepdims=True)
    return (x - m) / jnp.sqrt(v + eps)

def _scatter_add(tgt, idx, src, axis=0):
    return tgt.at[idx].add(src)

def _segment_sum(src, seg, n):
    return jax.ops.segment_sum(src, seg, n)
kernel_name = 'mk_gnn_resnorm_d2_gnn_r8_87b8c1'

def setup_inputs(seed: int=0):
    np.random.seed(seed)
    _w = jnp.asarray

    def _rec_inputs():
        import jax
        import jax.numpy as jnp
        _gk = jax.random.key(seed)
        x = -0.000202 + 1 * jax.random.normal(jax.random.fold_in(_gk, 1), (6250, 128), jnp.float32)
        _s = jax.random.randint(jax.random.fold_in(_gk, 2), (100000,), 0, 6250, jnp.int32)
        _d = jax.random.randint(jax.random.fold_in(_gk, 3), (100000,), 0, 6250, jnp.int32)
        _loop = jnp.arange(6250, dtype=jnp.int32)
        src = jnp.concatenate([_s, _d, _loop])
        dst = jnp.concatenate([_d, _s, _loop])
        _o = jnp.argsort(dst, stable=True)
        src = src[_o]
        dst = dst[_o]
        edge_type_5 = jax.random.randint(jax.random.fold_in(_gk, 12), (206250,), 0, 5, jnp.int32)
        edge_type_8 = jax.random.randint(jax.random.fold_in(_gk, 13), (206250,), 0, 8, jnp.int32)
        edge_weight1 = jax.random.uniform(jax.random.fold_in(_gk, 14), (206250, 1), jnp.float32, 0.0, 0.999998)
        return (x, src, dst, edge_type_5, edge_type_8, edge_weight1)
    x, src, dst, edge_type_5, edge_type_8, edge_weight1 = _rec_inputs()

    def _L0_gnn_setup():
        import jax, jax.numpy as jnp
        import numpy as np
        N_NODES = 6250
        N_EDGES = 100000
        N_RELS = 8
        D = 128

        def _rgcn_layer(h, W, src, dst, rel, norm, activation):
            t = jnp.einsum('nd,rdo->rno', h, W)
            msg = t[rel, src] * norm
            agg = jax.ops.segment_sum(msg, dst, num_segments=N_NODES)
            if activation is not None:
                agg = activation(agg)
            return agg
        key = jax.random.key(seed)
        ks = jax.random.split(key, 8)
        node_h = jax.random.normal(ks[0], (N_NODES, D), dtype=jnp.float32)
        src = jax.random.randint(ks[1], (N_EDGES,), 0, N_NODES, dtype=jnp.int32)
        dst = jax.random.randint(ks[2], (N_EDGES,), 0, N_NODES, dtype=jnp.int32)
        rel_type = jax.random.randint(ks[3], (N_EDGES,), 0, N_RELS, dtype=jnp.int32)
        norm = jax.random.uniform(ks[4], (N_EDGES, 1), dtype=jnp.float32)
        scale = 1.0 / np.sqrt(D)
        W_in = jax.random.normal(ks[5], (N_RELS, D, D), dtype=jnp.float32) * scale
        W_hid = jax.random.normal(ks[6], (N_RELS, D, D), dtype=jnp.float32) * scale
        W_out = jax.random.normal(ks[7], (N_RELS, D, D), dtype=jnp.float32) * scale
        return {'node_h': node_h, 'src': src, 'dst': dst, 'rel_type': rel_type, 'norm': norm, 'W_in': W_in, 'W_hid': W_hid, 'W_out': W_out}
    _L0_gnn_all = _L0_gnn_setup()
    _L0_gnn_in = {k: v for k, v in _L0_gnn_all.items() if k in ('W_in', 'W_hid', 'W_out')}
    del _L0_gnn_all

    def _L1_gnn_setup():
        import jax, jax.numpy as jnp
        import numpy as np
        N_NODES = 6250
        N_EDGES = 80000
        IN_FEAT = 128
        OUT_FEAT = 128
        N_REL = 5
        key = jax.random.key(seed)
        ks = jax.random.split(key, 8)
        x = jax.random.normal(ks[0], (N_NODES, IN_FEAT), dtype=jnp.float32)
        weight = jax.random.normal(ks[1], (N_REL, IN_FEAT, OUT_FEAT), dtype=jnp.float32) * (1.0 / np.sqrt(IN_FEAT))
        gate_weight = jax.random.normal(ks[2], (N_REL, IN_FEAT), dtype=jnp.float32) * (1.0 / np.sqrt(IN_FEAT))
        gate_bias = jax.random.normal(ks[3], (N_REL, 1), dtype=jnp.float32)
        bias = jax.random.normal(ks[4], (OUT_FEAT,), dtype=jnp.float32)
        src = jax.random.randint(ks[5], (N_EDGES,), 0, N_NODES, dtype=jnp.int64 if jax.config.jax_enable_x64 else jnp.int32)
        dst = jax.random.randint(ks[6], (N_EDGES,), 0, N_NODES, dtype=jnp.int64 if jax.config.jax_enable_x64 else jnp.int32)
        rel = jax.random.randint(ks[7], (N_EDGES,), 0, N_REL, dtype=jnp.int64 if jax.config.jax_enable_x64 else jnp.int32)
        return {'x': x, 'weight': weight, 'gate_weight': gate_weight, 'gate_bias': gate_bias, 'bias': bias, 'src': src, 'dst': dst, 'rel': rel}
    _L1_gnn_all = _L1_gnn_setup()
    _L1_gnn_in = {k: v for k, v in _L1_gnn_all.items() if k in ('weight', 'gate_weight', 'gate_bias', 'bias')}
    del _L1_gnn_all
    return {'x': x, 'src': src, 'dst': dst, 'edge_type_5': edge_type_5, 'edge_type_8': edge_type_8, 'edge_weight1': edge_weight1, 'L0_gnn_W_in': _L0_gnn_in['W_in'], 'L0_gnn_W_hid': _L0_gnn_in['W_hid'], 'L0_gnn_W_out': _L0_gnn_in['W_out'], 'L1_gnn_weight': _L1_gnn_in['weight'], 'L1_gnn_gate_weight': _L1_gnn_in['gate_weight'], 'L1_gnn_gate_bias': _L1_gnn_in['gate_bias'], 'L1_gnn_bias': _L1_gnn_in['bias']}

def reference(x, src, dst, edge_type_5, edge_type_8, edge_weight1, L0_gnn_W_in, L0_gnn_W_hid, L0_gnn_W_out, L1_gnn_weight, L1_gnn_gate_weight, L1_gnn_gate_bias, L1_gnn_bias):
    import jax
    import jax.numpy as jnp

    def _L0_gnn_ref(node_h, src, dst, rel_type, norm, W_in, W_hid, W_out):
        import jax, jax.numpy as jnp
        import numpy as np
        N_NODES = 6250
        N_EDGES = 100000
        N_RELS = 8
        D = 128

        def _rgcn_layer(h, W, src, dst, rel, norm, activation):
            t = jnp.einsum('nd,rdo->rno', h, W)
            msg = t[rel, src] * norm
            agg = jax.ops.segment_sum(msg, dst, num_segments=N_NODES)
            if activation is not None:
                agg = activation(agg)
            return agg
        h = _rgcn_layer(node_h, W_in, src, dst, rel_type, norm, jax.nn.relu)
        h = _rgcn_layer(h, W_hid, src, dst, rel_type, norm, jax.nn.relu)
        h = _rgcn_layer(h, W_out, src, dst, rel_type, norm, None)
        return h

    def _L1_gnn_ref(x, weight, gate_weight, gate_bias, bias, src, dst, rel):
        import jax, jax.numpy as jnp
        import numpy as np
        N_NODES = 6250
        N_EDGES = 80000
        IN_FEAT = 128
        OUT_FEAT = 128
        N_REL = 5
        n_nodes = x.shape[0]
        h_all = jnp.einsum('ni,rio->rno', x, weight)
        msg = h_all[rel, src]
        gate_all = x @ gate_weight.T
        score = jax.nn.sigmoid(gate_all[src, rel] + gate_bias[rel, 0])
        msg = score[:, None] * msg
        h = jax.ops.segment_sum(msg, dst, num_segments=n_nodes)
        h = h + bias
        return jax.nn.relu(h)
    x = _layernorm(x + _L0_gnn_ref(x, src, dst, edge_type_8, edge_weight1, L0_gnn_W_in, L0_gnn_W_hid, L0_gnn_W_out), axis=-1)
    x = _layernorm(x + _L1_gnn_ref(x, L1_gnn_weight, L1_gnn_gate_weight, L1_gnn_gate_bias, L1_gnn_bias, src, dst, edge_type_5), axis=-1)
    return x

_drawn_inputs = setup_inputs


def setup_inputs(seed=0):
    import zlib

    import numpy as np

    out = dict(_drawn_inputs(seed))
    spreads = {}
    factors = {}
    for name, (base, spread) in spreads.items():
        noise = np.random.default_rng([zlib.crc32(name.encode()), seed]).standard_normal(out[name].shape)
        drawn = base * np.exp(spread * noise) if base else spread * noise
        out[name] = jnp.asarray(drawn.astype(out[name].dtype))
    for name, factor in factors.items():
        out[name] = (out[name] * factor).astype(out[name].dtype)
    return out
```

```python
import concourse.bass as bass
from concourse import mybir
from contextlib import ExitStack

f32 = mybir.dt.float32
i32 = mybir.dt.int32
ALU = mybir.AluOpType
ACT = mybir.ActivationFunctionType
AX = mybir.AxisListType

P = 128
N_NODES = 6250
N_EDGES = 206250
D = 128
R0, R1 = 8, 5
SLOTS_PER_NODE = 8
LAYERS = 4
GATED = 3
TW = 13
HALVES = 2
TI = TW * HALVES
GROUP = TW * P
ITERS = -(-N_EDGES // (TI * P))
GROUPS = ITERS * HALVES
WIN = 64
BLOCK = 100
BLOCKS = -(-N_NODES // BLOCK)
NPAD = BLOCKS * BLOCK
LAST_ROWS = N_NODES - (BLOCKS - 1) * BLOCK
LAG = 2
MAIN_BLOCKS = ITERS - LAG
CHUNK = 1664
NCHUNK = 4
CW = CHUNK // 4
SUMS = CHUNK * NCHUNK
EPS = 1e-5
GCOLS = R1 * D + R1

FULL_GROUPS = N_EDGES // GROUP
LEFT = N_EDGES - FULL_GROUPS * GROUP
LEFT_P, LEFT_J = LEFT // TW, LEFT % TW

USES0_FIRST, USES1_FIRST = (BLOCKS + 1) // 2, BLOCKS // 2
TAIL = list(range(MAIN_BLOCKS, BLOCKS))
TAIL_BUF = [(i + 1) % 2 for i in range(len(TAIL))]
USES0_LAYER = MAIN_BLOCKS + TAIL_BUF.count(0)
USES1_LAYER = TAIL_BUF.count(1)

assert SUMS >= NPAD and SUMS >= N_NODES + WIN and ITERS * TI * P - N_EDGES < GROUP
assert FULL_GROUPS == GROUPS - 1


def gnn_program(nc, x, src, dst, type5, type8, edge_w, w_in, w_hid, w_out, w_gated, gate_w, gate_b, bias, out):
    tables = [nc.dram_tensor(f"table{i}", (NPAD * SLOTS_PER_NODE, D), f32, kind="Internal").ap() for i in range(2)]
    table_rows = [t.rearrange("(n r) o -> n (r o)", r=SLOTS_PER_NODE) for t in tables]

    with ExitStack() as ctx:
        def sb(name, shape, dt=f32):
            return ctx.enter_context(nc.sbuf_tensor(name, shape, dt))

        def ps(name, shape, dt=f32):
            return ctx.enter_context(nc.psum_tensor(name, shape, dt))

        def sem(name):
            return ctx.enter_context(nc.semaphore(name))

        sums = sb("sums", [P, SUMS])
        residual = sb("residual", [P, NPAD])
        src_i = sb("src_i", [P, GROUPS, TW], i32)
        dst_i = sb("dst_i", [P, GROUPS, TW], i32)
        type_i = [sb(f"type{r}_i", [P, GROUPS, TW], i32) for r in (R0, R1)]
        row_of = [sb(f"row_of_{r}", [P, GROUPS, TW]) for r in (R0, R1)]
        weight_of = [sb("edge_weight", [P, GROUPS, TW]), sb("one_weight", [P, GROUPS, TW])]
        dst_of = sb("dst_of", [P, GROUPS, 2, TW])
        base_row = sb("base_row", [1, GROUPS], i32)
        base_all = sb("base_all", [P, GROUPS], i32)
        base_least = sb("base_least", [P, ITERS, HALVES], i32)
        base_f = sb("base_f", [P, GROUPS])
        base_least_f = sb("base_least_f", [P, GROUPS])
        src_row = sb("src_row", [P, GROUPS, TW])
        base_over = sb("base_over", [P, GROUPS])
        checks = sb("checks", [P, 6])
        bad_edges = sb("bad_edges", [P, 1])
        spread_ok = sb("spread_ok", [1, 1], i32)
        ones_col = sb("ones_col", [P, 1])
        eps_col = sb("eps_col", [P, 1])
        iota_i = sb("iota_i", [P, CHUNK], i32)
        iota_f = sb("iota_f", [P, CHUNK])
        ident = sb("ident", [P, P])
        rows_now = [sb(f"rows_now{v}", [P, TW], i32) for v in range(HALVES)]
        weight_now = [sb(f"weight_now{v}", [P, TW]) for v in range(HALVES)]
        dst_now = [sb(f"dst_now{v}", [P, 2, TW]) for v in range(HALVES)]
        gathered = sb("gathered", [P, TI, D])
        onehot = [sb(f"onehot{v}", [P, TW, WIN]) for v in range(HALVES)]
        dst_shift = sb("dst_shift", [P, NCHUNK, TW])
        wide_onehot = sb("wide_onehot", [P, CHUNK])
        weights = [sb(f"weights{i}", [P, SLOTS_PER_NODE * D]) for i in range(3)]
        weights.append(sb("weights3", [P, GCOLS]))
        bias_col = sb("bias_col", [P, 1])
        gate_b_row = sb("gate_b_row", [1, R1])
        gate_b_all = sb("gate_b_all", [P, R1])
        x_in = [sb(f"x_in{i}", [BLOCK, D]) for i in range(2)]
        h_t = [sb(f"h_t{i}", [P, BLOCK]) for i in range(2)]
        relu_t = sb("relu_t", [P, BLOCK])
        y_t = [sb(f"y_t{i}", [P, BLOCK]) for i in range(2)]
        norm = [sb(f"norm{i}", [BLOCK, D]) for i in range(2)]
        stats = sb("stats", [BLOCK, 6])
        mean_var = sb("mean_var", [BLOCK, 2])
        std = sb("std", [BLOCK, 1])
        rstd = sb("rstd", [BLOCK, 1])
        logits = sb("logits", [BLOCK, R1])
        gates = sb("gates", [BLOCK, R1])
        rows_out = [sb(f"rows_out{i}", [BLOCK, SLOTS_PER_NODE * D]) for i in range(2)]

        window = [ps(f"window{v}", [P, 512]) for v in range(HALVES)]
        product = ps("product", [P, 4, 512])
        turned = ps("turned", [P, 512])
        x_turns = [turned, window[0]]
        iota_ps = ps("iota_ps", [P, 512])

        edges_loaded = sem("edges_loaded")
        first_loaded = sem("first_loaded")
        weights_loaded = sem("weights_loaded")
        consts_made = sem("consts_made")
        index_step = sem("index_step")
        weight_cleared = sem("weight_cleared")
        x_loaded = [sem(f"x_loaded{i}") for i in range(2)]
        x_cleared = sem("x_cleared")
        x_turned = sem("x_turned")
        h_ready = sem("h_ready")
        residual_kept = sem("residual_kept")
        multiplied = sem("multiplied")
        rows_ready = sem("rows_ready")
        rows_stored = [sem(f"rows_stored{i}") for i in range(2)]
        check_step = sem("check_step")
        check_summed = sem("check_summed")
        iota_placed = sem("iota_placed")
        rows_staged = [sem(f"rows_staged{v}") for v in range(HALVES)]
        edges_staged = sem("edges_staged")
        landed = [sem(f"landed{s}") for s in range(TI)]
        windows_begun = sem("windows_begun")
        tiles_summed = sem("tiles_summed")
        onehots_ready = sem("onehots_ready")
        windows_added = sem("windows_added")
        sums_cleared = sem("sums_cleared")
        block_read = sem("block_read")
        relu_ready = sem("relu_ready")
        y_ready = sem("y_ready")
        y_turned = sem("y_turned")
        variance_ready = sem("variance_ready")
        rstd_ready = sem("rstd_ready")
        std_ready = sem("std_ready")
        norm_ready = sem("norm_ready")
        norm_turned = sem("norm_turned")
        logits_ready = sem("logits_ready")
        gates_ready = sem("gates_ready")
        out_stored = [sem(f"out_stored{i}") for i in range(2)]
        shifted = sem("shifted")
        wide_ready = sem("wide_ready")
        wide_summed = sem("wide_summed")
        wide_added = sem("wide_added")

        EDGE_DMAS = 4 * 5 + 3 + 1
        WEIGHT_DMAS = 6

        def block_number(layer, b):
            return BLOCKS * (layer + 1) + b

        def norm_number(layer, b):
            return BLOCKS * (layer - 2) + b

        def buffer_uses(layer, b, buf):
            if buf == 0:
                within = b if not isinstance(b, int) or b < MAIN_BLOCKS else MAIN_BLOCKS + TAIL_BUF[:b - MAIN_BLOCKS].count(0)
                return USES0_FIRST + USES0_LAYER * layer + within
            return USES1_FIRST + USES1_LAYER * layer + TAIL_BUF[:b - MAIN_BLOCKS].count(1)

        def out_uses(b, buf):
            if buf == 0:
                return b if not isinstance(b, int) or b < MAIN_BLOCKS else MAIN_BLOCKS + TAIL_BUF[:b - MAIN_BLOCKS].count(0)
            return TAIL_BUF[:b - MAIN_BLOCKS].count(1)

        def nodes(b):
            return bass.ds(b * BLOCK, BLOCK)

        def load_edges(eng, to, array, fill):
            full, left = FULL_GROUPS * GROUP, LEFT_P * TW
            eng.dma_start(to[:, 0:FULL_GROUPS, :],
                          array[0:full].rearrange("(g p j) -> p g j", p=P, j=TW)).then_inc(edges_loaded, 16)
            eng.dma_start(to[0:LEFT_P, FULL_GROUPS, :],
                          array[full:full + left].rearrange("(p j) -> p j", j=TW)).then_inc(edges_loaded, 16)
            eng.dma_start(to[LEFT_P:LEFT_P + 1, FULL_GROUPS, 0:LEFT_J],
                          array[full + left:N_EDGES].rearrange("(p j) -> p j", p=1)).then_inc(edges_loaded, 16)
            if fill:
                eng.dma_start(to[LEFT_P:LEFT_P + 1, FULL_GROUPS, LEFT_J:TW],
                              array[N_EDGES - (TW - LEFT_J):N_EDGES].rearrange("(p j) -> p j", p=1)
                              ).then_inc(edges_loaded, 16)
                eng.dma_start(to[LEFT_P + 1:P, FULL_GROUPS, :],
                              array[N_EDGES - (P - LEFT_P - 1) * TW:N_EDGES].rearrange("(p j) -> p j", j=TW)
                              ).then_inc(edges_loaded, 16)

        block = ctx.enter_context(nc.Block())

        @block.sync
        def _(sp):
            def load_x(b, buf, rows=BLOCK):
                sp.dma_start(x_in[buf][0:rows, :], x[bass.ds(b * BLOCK, rows), :]).then_inc(x_loaded[buf], 16)

            def store_rows(layer, b, buf):
                sp.wait_ge(rows_ready, block_number(layer, b) + 1)
                cols = R1 * D if layer + 1 == GATED else SLOTS_PER_NODE * D
                sp.dma_start(table_rows[(layer + 1) % 2][nodes(b), 0:cols],
                             rows_out[buf][:, 0:cols]).then_inc(rows_stored[buf], 16)

            def store_out(b, buf, rows=BLOCK):
                sp.wait_ge(norm_ready, norm_number(GATED, b) + 1)
                sp.dma_start(out[bass.ds(b * BLOCK, rows), :], norm[buf][0:rows, :]).then_inc(out_stored[buf], 16)

            load_x(0, 0)
            load_x(1, 1)
            sp.dma_start(weights[0][:, :].rearrange("d (r o) -> d r o", r=R0),
                         w_in.rearrange("r d o -> d r o")).then_inc(first_loaded, 16)
            load_edges(sp, dst_i, dst, True)
            sp.wait_ge(weight_cleared, 1)
            load_edges(sp, weight_of[0], edge_w.rearrange("e o -> (e o)"), False)
            load_edges(sp, type_i[1], type5, True)
            for to, w in ((weights[1], w_hid), (weights[2], w_out)):
                sp.dma_start(to[:, :].rearrange("d (r o) -> d r o", r=R0),
                             w.rearrange("r d o -> d r o")).then_inc(weights_loaded, 16)
            sp.dma_start(weights[3][:, 0:R1 * D].rearrange("d (r o) -> d r o", r=R1),
                         w_gated.rearrange("r d o -> d r o")).then_inc(weights_loaded, 16)
            with nc.allow_non_contiguous_dma(reason="small transposed vectors"):
                sp.dma_start(weights[3][:, R1 * D:GCOLS], gate_w.rearrange("r d -> d r")).then_inc(weights_loaded, 16)
                sp.dma_start(bias_col[:, :], bias.rearrange("(d o) -> d o", o=1)).then_inc(weights_loaded, 16)
                sp.dma_start(gate_b_row[:, :], gate_b.rearrange("r o -> o r")).then_inc(weights_loaded, 16)
            with sp.Fori(0, BLOCKS // 2 - 1) as i:
                sp.wait_ge(x_turned, 2 * i + 1)
                load_x(2 * i + 2, 0)
                sp.wait_ge(x_turned, 2 * i + 2)
                load_x(2 * i + 3, 1)
                for buf in range(2):
                    store_rows(-1, 2 * i + buf, buf)
            sp.wait_ge(x_turned, BLOCKS - 2)
            sp.wait_ge(x_cleared, 1)
            load_x(BLOCKS - 1, 0, LAST_ROWS)
            for b in range(BLOCKS - 3, BLOCKS):
                store_rows(-1, b, b % 2)

            for layer in range(LAYERS - 1):
                with sp.Fori(0, MAIN_BLOCKS) as b:
                    store_rows(layer, b, 0)
                for b, buf in zip(TAIL, TAIL_BUF):
                    store_rows(layer, b, buf)
            with sp.Fori(0, MAIN_BLOCKS) as b:
                store_out(b, 0)
            for b, buf in zip(TAIL, TAIL_BUF):
                store_out(b, buf, LAST_ROWS if b == BLOCKS - 1 else BLOCK)
            sp.wait_ge(out_stored[0], 16 * USES0_LAYER)
            sp.wait_ge(out_stored[1], 16 * USES1_LAYER)

        @block.gpsimd
        def _(pool):
            nc.gpsimd.iota(iota_i[:, :], pattern=[[1, CHUNK]], base=0, channel_multiplier=0).then_inc(consts_made, 1)
            nc.gpsimd.iota(base_least[:, :, :], pattern=[[BLOCK, ITERS], [0, HALVES]], base=-BLOCK * (LAG - 1),
                           channel_multiplier=0).then_inc(consts_made, 1)
            nc.gpsimd.memset(ident[:, :], 0.0).then_inc(consts_made, 1)
            nc.gpsimd.memset(weight_of[1][:, :, :], 1.0).then_inc(consts_made, 1)
            pool.wait_ge(consts_made, 4)
            nc.gpsimd.tensor_copy(iota_f[:, :], iota_i[:, :]).then_inc(consts_made, 1)
            nc.gpsimd.affine_select(out=ident[:, :], in_=ident[:, :], compare_op=ALU.not_equal, fill=1.0,
                                    base=0, pattern=[[-1, P]], channel_multiplier=1).then_inc(consts_made, 1)
            nc.gpsimd.affine_select(out=weight_of[1][:, GROUPS - 1, :], in_=weight_of[1][:, GROUPS - 1, :],
                                    compare_op=ALU.is_ge, fill=0.0, base=LEFT - 1, pattern=[[-1, TW]],
                                    channel_multiplier=-TW).then_inc(consts_made, 1)
            pool.wait_ge(weights_loaded, 16 * WEIGHT_DMAS)
            nc.gpsimd.partition_broadcast(gate_b_all[:, :], gate_b_row[:, :]).then_inc(consts_made, 1)
            pool.wait_ge(edges_loaded, 16 * EDGE_DMAS)
            nc.gpsimd.partition_broadcast(base_all[:, :], base_row[:, :]).then_inc(index_step, 1)
            nc.gpsimd.tensor_scalar(src_row[:, :, :], src_i[:, :, :], float(SLOTS_PER_NODE), None,
                                    ALU.mult).then_inc(index_step, 1)
            for k in range(2):
                nc.gpsimd.tensor_copy(row_of[k][:, :, :], type_i[k][:, :, :]).then_inc(index_step, 1)
            nc.gpsimd.tensor_copy(dst_of[:, :, 1, :], dst_i[:, :, :]).then_inc(index_step, 1)
            nc.gpsimd.tensor_copy(base_least_f[:, :], base_least[:, :, :].rearrange("p a b -> p (a b)")
                                  ).then_inc(index_step, 1)
            pool.wait_ge(index_step, 6)
            nc.gpsimd.tensor_copy(base_f[:, :], base_all[:, :]).then_inc(index_step, 1)
            for k in range(2):
                nc.gpsimd.tensor_tensor(row_of[k][:, :, :], row_of[k][:, :, :], src_row[:, :, :],
                                        ALU.add).then_inc(index_step, 1)
            pool.wait_ge(index_step, 9)
            nc.gpsimd.tensor_tensor(dst_of[:, :, 0, :], dst_of[:, :, 1, :],
                                    base_f[:, :].unsqueeze(2).to_broadcast([P, GROUPS, TW]),
                                    ALU.subtract).then_inc(index_step, 1)
            nc.gpsimd.tensor_tensor(base_over[:, :], base_f[:, :], base_least_f[:, :],
                                    ALU.subtract).then_inc(index_step, 1)

            for layer in range(LAYERS):
                pool.wait_ge(rows_stored[0], 16 * (USES0_FIRST + USES0_LAYER * layer))
                pool.wait_ge(rows_stored[1], 16 * (USES1_FIRST + USES1_LAYER * layer))
                with pool.Fori(0, ITERS) as t:
                    for v in range(HALVES):
                        pool.wait_ge(rows_staged[v], t + (layer * ITERS + 1))
                        pool.sem_inc(windows_begun, 1)
                        for j in range(TW):
                            nc.gpsimd.indirect_dma_start(
                                gathered[:, v * TW + j, :], None, tables[layer % 2],
                                bass.IndirectOffsetOnAxis(ap=rows_now[v][:, j:j + 1], axis=0)
                                ).then_inc(landed[v * TW + j], 16)

        @block.scalar
        def _(act):
            load_edges(act, src_i, src, True)
            load_edges(act, type_i[0], type8, True)
            with nc.allow_non_contiguous_dma(reason="first destination of each window"):
                act.dma_start(base_row[0:1, :], dst.rearrange("(o e) -> o e", o=1)[:, 0:N_EDGES:GROUP]
                              ).then_inc(edges_loaded, 16)

            def rows_from_product(layer, n, uses, buf):
                act.wait_ge(multiplied, n + 1)
                if uses is not None:
                    act.wait_ge(rows_stored[buf], 16 * uses)
                if layer + 1 == GATED:
                    act.wait_ge(logits_ready, norm_number(layer, n - BLOCKS * (layer + 1)) + 1)
                    nc.scalar.activation(gates[:, :], logits[:, :], ACT.Sigmoid).then_inc(gates_ready, 1)
                    act.wait_ge(gates_ready, norm_number(layer, n - BLOCKS * (layer + 1)) + 1)
                    for r in range(R1):
                        last = nc.scalar.activation(rows_out[buf][:, r * D:(r + 1) * D],
                                                    product[0:BLOCK, 2 * buf + r // 4, (r % 4) * D:(r % 4 + 1) * D],
                                                    ACT.Copy, scale=gates[:, r:r + 1])
                else:
                    last = nc.scalar.activation(rows_out[buf][:, :].rearrange("p (a b) -> p a b", a=2),
                                                product[0:BLOCK, 2 * buf:2 * buf + 2, :], ACT.Copy)
                last.then_inc(rows_ready, 1)

            for b in range(2):
                rows_from_product(-1, b, None, b)
            with act.Fori(1, BLOCKS // 2) as i:
                for buf in range(2):
                    rows_from_product(-1, 2 * i + buf, i, buf)
            rows_from_product(-1, BLOCKS - 1, BLOCKS // 2, 0)

            def turn_block(layer, b, buf, added):
                n = block_number(layer, b)
                if layer < 2:
                    act.wait_ge(windows_added, added)
                    nc.scalar.activation(h_t[buf][:, :], sums[:, nodes(b)], ACT.Relu).then_inc(h_ready, 1)
                    rows_from_product(layer, n, buffer_uses(layer, b, buf), buf)
                else:
                    m = norm_number(layer, b)
                    if layer == GATED:
                        act.wait_ge(windows_added, added)
                        act.wait_ge(y_ready, m)
                        nc.scalar.activation(relu_t[:, :], sums[:, nodes(b)], ACT.Relu,
                                             bias=bias_col[:, 0:1]).then_inc(relu_ready, 1)
                    act.wait_ge(variance_ready, m + 1)
                    nc.scalar.activation(std[:, :], mean_var[:, 1:2], ACT.Sqrt,
                                         bias=eps_col[0:BLOCK, 0:1]).then_inc(std_ready, 1)
                    if layer + 1 == GATED:
                        act.wait_ge(norm_turned, m + 1)
                        nc.scalar.activation(h_t[buf][:, :], turned[:, P:P + BLOCK], ACT.Copy).then_inc(h_ready, 1)
                        rows_from_product(layer, n, buffer_uses(layer, b, buf), buf)

            act.wait_ge(weights_loaded, 16 * WEIGHT_DMAS)
            act.wait_ge(check_step, 1)
            for layer in range(LAYERS):
                base = 2 + layer * GROUPS
                with act.Fori(0, MAIN_BLOCKS) as b:
                    turn_block(layer, b, 0, (b + LAG) * HALVES + base)
                for b, buf in zip(TAIL, TAIL_BUF):
                    turn_block(layer, b, buf, base + GROUPS)

        @block.vector
        def _(dve):
            nc.vector.memset(weight_of[0][:, GROUPS - 1, :], 0.0).then_inc(weight_cleared, 1)
            nc.vector.memset(ones_col[:, :], 1.0).then_inc(check_step, 1)
            nc.vector.memset(eps_col[:, :], EPS)
            dve.sem_inc(windows_added, 2)

            def keep_x(n, buf):
                dve.wait_ge(x_turned, n + 1)
                nc.vector.tensor_copy(h_t[buf][:, :], x_turns[buf][:, 0:BLOCK]).then_inc(h_ready, 1)
                nc.vector.tensor_copy(residual[:, nodes(n)], x_turns[buf][:, 0:BLOCK]).then_inc(residual_kept, 1)

            keep_x(0, 0)
            keep_x(1, 1)
            with dve.Fori(1, BLOCKS // 2) as i:
                for buf in range(2):
                    dve.wait_ge(multiplied, 2 * i + buf - 1)
                    keep_x(2 * i + buf, buf)
            nc.vector.memset(x_in[0][:, :], 0.0).then_inc(x_cleared, 1)
            dve.wait_ge(multiplied, BLOCKS - 2)
            keep_x(BLOCKS - 1, 0)

            dve.wait_ge(index_step, 11)
            dve.wait_ge(consts_made, 8)
            nc.vector.tensor_copy(iota_ps[:, 0:WIN], iota_f[:, 0:WIN]).then_inc(iota_placed, 1)
            inside = dst_of[:, :, 0, :]
            nc.vector.tensor_reduce(checks[:, 0:1], inside, AX.XY, ALU.max).then_inc(check_step, 1)
            nc.vector.tensor_reduce(checks[:, 1:2], inside, AX.XY, ALU.min).then_inc(check_step, 1)
            nc.vector.tensor_reduce(checks[:, 2:3], base_over[:, :], AX.X, ALU.min).then_inc(check_step, 1)
            dve.wait_ge(check_step, 4)
            nc.vector.tensor_scalar(checks[:, 3:4], checks[:, 0:1], float(WIN), None, ALU.is_ge).then_inc(check_step, 1)
            nc.vector.tensor_scalar(checks[:, 4:6], checks[:, 1:3], 0.0, None, ALU.is_lt).then_inc(check_step, 1)
            dve.wait_ge(check_step, 6)
            nc.vector.tensor_reduce(bad_edges[:, :], checks[:, 3:6], AX.X, ALU.add).then_inc(check_step, 1)
            dve.wait_ge(check_summed, 1)
            nc.vector.tensor_scalar(spread_ok[:, :], iota_ps[0:1, 256:257], 0.0, None, ALU.is_equal
                                    ).then_inc(check_step, 1)
            dve.wait_ge(check_step, 8)

            def stage(layer, t, v):
                g, kind = t * HALVES + v, int(layer == GATED)
                nc.vector.tensor_copy(rows_now[v][:, :], row_of[kind][:, bass.ds(g, 1), :].rearrange("p a j -> p (a j)")
                                      ).then_inc(rows_staged[v], 1)
                nc.vector.tensor_copy(weight_now[v][:, :],
                                      weight_of[kind][:, bass.ds(g, 1), :].rearrange("p a j -> p (a j)"))
                nc.vector.tensor_copy(dst_now[v][:, :, :],
                                      dst_of[:, bass.ds(g, 1), :, :].rearrange("p a c j -> p (a c) j")
                                      ).then_inc(edges_staged, 1)

            def read_y(layer, b, buf):
                m = norm_number(layer, b)
                if layer == GATED:
                    dve.wait_ge(relu_ready, m - BLOCKS + 1)
                    nc.vector.tensor_tensor(y_t[buf][:, :], relu_t[:, :], residual[:, nodes(b)], ALU.add
                                            ).then_inc(y_ready, 1)
                else:
                    nc.vector.tensor_tensor(y_t[buf][:, :], sums[:, nodes(b)], residual[:, nodes(b)], ALU.add
                                            ).then_inc(y_ready, 1)

            def layernorm(layer, b, buf):
                m = norm_number(layer, b)
                dve.wait_ge(y_turned, m + 1)
                nc.vector.bn_stats(stats[:, :], turned[0:BLOCK, 0:D])
                dve.drain()
                nc.vector.bn_aggr(mean_var[:, :], stats[:, :]).then_inc(variance_ready, 1)
                dve.wait_ge(std_ready, m + 1)
                nc.vector.reciprocal(rstd[:, :], std[:, :]).then_inc(rstd_ready, 1)
                dve.wait_ge(rstd_ready, m + 1)
                if layer == GATED and not (isinstance(b, int) and out_uses(b, buf) == 0):
                    dve.wait_ge(out_stored[buf], 16 * out_uses(b, buf))
                nc.vector.tensor_scalar(norm[buf][:, :], turned[0:BLOCK, 0:D], mean_var[:, 0:1], rstd[:, 0:1],
                                        ALU.subtract, ALU.mult).then_inc(norm_ready, 1)

            def gate_logits(layer, b, buf):
                m, n = norm_number(layer, b), block_number(layer, b)
                dve.wait_ge(multiplied, n + 1)
                nc.vector.tensor_tensor(logits[:, :], product[0:BLOCK, 2 * buf + 1, D:D + R1],
                                        gate_b_all[0:BLOCK, :], ALU.add).then_inc(logits_ready, 1)
                nc.vector.tensor_copy(residual[:, nodes(b)], h_t[buf][:, :]).then_inc(residual_kept, 1)

            def tail_block(layer, b, buf):
                if layer >= 2:
                    read_y(layer, b, buf)
                    layernorm(layer, b, buf)
                if layer == 2:
                    gate_logits(layer, b, buf)

            def clear_sums(layer):
                if layer in (1, 2):
                    dve.wait_ge(h_ready, BLOCKS * (layer + 1))
                if layer == GATED:
                    dve.wait_ge(y_ready, BLOCKS)
                nc.vector.memset(sums[:, :], 0.0).then_inc(sums_cleared, 1)
                dve.wait_ge(sums_cleared, layer + 1)

            def sorted_layer(layer):
                k0 = layer * GROUPS

                def onehots(k, v):
                    dve.wait_ge(edges_staged, k + 1)
                    for j in range(TW):
                        last = nc.vector.tensor_scalar(onehot[v][:, j, :], iota_ps[:, 0:WIN], dst_now[v][:, 0, j:j + 1],
                                                       weight_now[v][:, j:j + 1], ALU.is_equal, ALU.mult)
                    last.then_inc(onehots_ready, 1)

                def add_window(t, k, v):
                    start = dve.value_load(base_row[0:1, bass.ds(t * HALVES + v, 1)], min_val=0, max_val=N_NODES - 1)
                    dve.wait_ge(tiles_summed, (k - k0) * TW + (layer * ITERS * TI + TW))
                    dve.wait_ge(windows_added, k + 2)
                    at = sums[:, bass.ds(start, WIN)]
                    nc.vector.tensor_tensor(at, at, window[v][:, 0:WIN], ALU.add).then_inc(windows_added, 1)

                def iteration(t, b, last=False):
                    k = t * HALVES + k0
                    onehots(k + 1, 1)
                    if b is not None and layer >= 2:
                        if layer == 2:
                            dve.wait_ge(windows_added, k + 2)
                        read_y(layer, b, 0)
                    add_window(t, k, 0)
                    if not last:
                        stage(layer, t + 1, 0)
                        onehots(k + 2, 0)
                    if b is not None and layer >= 2:
                        layernorm(layer, b, 0)
                    if b is not None and layer == 2:
                        gate_logits(layer, b, 0)
                    add_window(t, k + 1, 1)
                    if not last:
                        stage(layer, t + 1, 1)

                stage(layer, 0, 0)
                stage(layer, 0, 1)
                onehots(k0, 0)
                clear_sums(layer)
                with dve.Fori(0, LAG) as t:
                    iteration(t, None)
                iteration(LAG, 0)
                with dve.Fori(LAG + 1, ITERS - 1) as t:
                    iteration(t, t - LAG)
                iteration(ITERS - 1, ITERS - 1 - LAG, last=True)
                if layer == 2:
                    dve.wait_ge(windows_added, 2 + k0 + GROUPS)
                for b, buf in zip(TAIL, TAIL_BUF):
                    tail_block(layer, b, buf)

            def unsorted_layer(layer):
                k0, n0 = layer * GROUPS, layer * ITERS * TI
                clear_sums(layer)
                with dve.Fori(0, ITERS) as t:
                    for v in range(HALVES):
                        if v == 0:
                            for u in range(HALVES):
                                stage(layer, t, u)
                        dve.wait_ge(edges_staged, (t + 1) * HALVES + k0)
                        for q in range(NCHUNK):
                            last = nc.vector.tensor_scalar(dst_shift[:, q, :], dst_now[v][:, 1, :], float(-q * CHUNK),
                                                           None, ALU.add)
                        last.then_inc(shifted, 1)
                        dve.wait_ge(shifted, t * HALVES + (k0 + v + 1))
                        for j in range(TW):
                            for q in range(NCHUNK):
                                m = t * (TI * NCHUNK) + ((n0 + v * TW + j) * NCHUNK + q)
                                nc.vector.tensor_scalar(wide_onehot[:, :], iota_f[:, :], dst_shift[:, q, j:j + 1],
                                                        weight_now[v][:, j:j + 1], ALU.is_equal, ALU.mult
                                                        ).then_inc(wide_ready, 1)
                                dve.wait_ge(wide_summed, m + 1)
                                at = sums[:, q * CHUNK:(q + 1) * CHUNK].rearrange("p (a b) -> p a b", a=4)
                                nc.vector.tensor_tensor(at, at, product[:, :, 0:CW], ALU.add).then_inc(wide_added, 1)
                dve.wait_ge(wide_added, (layer + 1) * ITERS * TI * NCHUNK)
                dve.sem_inc(windows_added, GROUPS)
                if layer >= 2:
                    tail_block(layer, 0, 0)
                    with dve.Fori(1, MAIN_BLOCKS) as b:
                        tail_block(layer, b, 0)
                for b, buf in zip(TAIL, TAIL_BUF):
                    tail_block(layer, b, buf)

            flag = dve.value_load(spread_ok[0:1, 0:1], min_val=0, max_val=1)
            with dve.If(flag > 0):
                for layer in range(LAYERS):
                    sorted_layer(layer)
            with dve.Else():
                for layer in range(LAYERS):
                    unsorted_layer(layer)

        @block.tensor
        def _(pe):
            def turn_x(n, buf, uses, rows=BLOCK):
                pe.wait_ge(x_loaded[buf], 16 * (uses + 1))
                nc.tensor.transpose(x_turns[buf][:, 0:BLOCK], x_in[buf][:, :],
                                    ident[0:BLOCK, 0:BLOCK]).then_inc(x_turned, 1)

            def multiply(layer, n, buf):
                pe.wait_ge(h_ready, n + 1)
                w = weights[layer + 1]
                cols = GCOLS if layer + 1 == GATED else SLOTS_PER_NODE * D
                nc.tensor.matmul(product[0:BLOCK, 2 * buf, :], h_t[buf][:, :], w[:, 0:512], start=True, stop=True)
                nc.tensor.matmul(product[0:BLOCK, 2 * buf + 1, 0:cols - 512], h_t[buf][:, :], w[:, 512:cols],
                                 start=True, stop=True).then_inc(multiplied, 1)

            pe.wait_ge(consts_made, 7)
            turn_x(0, 0, 0)
            turn_x(1, 1, 0)
            pe.wait_ge(first_loaded, 16)
            multiply(-1, 0, 0)
            multiply(-1, 1, 1)
            with pe.Fori(1, BLOCKS // 2) as i:
                for buf in range(2):
                    pe.wait_ge(residual_kept, 2 * i + (buf - 1))
                    turn_x(2 * i + buf, buf, i)
                for buf in range(2):
                    pe.wait_ge(rows_ready, 2 * i + (buf - 1))
                    multiply(-1, 2 * i + buf, buf)
            pe.wait_ge(residual_kept, BLOCKS - 2)
            turn_x(BLOCKS - 1, 0, BLOCKS // 2)
            pe.wait_ge(rows_ready, BLOCKS - 2)
            multiply(-1, BLOCKS - 1, 0)

            pe.wait_ge(weights_loaded, 16 * WEIGHT_DMAS)
            pe.wait_ge(check_step, 7)
            nc.tensor.matmul(iota_ps[0:1, 256:257], bad_edges[:, :], ones_col[:, :], start=True, stop=True
                             ).then_inc(check_summed, 1)

            def turn_y(layer, b, buf):
                m = norm_number(layer, b)
                pe.wait_ge(y_ready, m + 1)
                nc.tensor.transpose(turned[0:BLOCK, 0:D], y_t[buf][:, :], ident[:, :]).then_inc(y_turned, 1)

            def turn_norm(layer, b, buf):
                m = norm_number(layer, b)
                pe.wait_ge(norm_ready, m + 1)
                nc.tensor.transpose(turned[:, P:P + BLOCK], norm[buf][:, :], ident[0:BLOCK, 0:BLOCK]
                                    ).then_inc(norm_turned, 1)

            def multiply_block(layer, b, buf):
                n = block_number(layer, b)
                pe.wait_ge(rows_ready, n)
                multiply(layer, n, buf)

            def tail_block(layer, b, buf):
                if layer >= 2:
                    turn_y(layer, b, buf)
                if layer == 2:
                    turn_norm(layer, b, buf)
                if layer < GATED:
                    multiply_block(layer, b, buf)

            def sorted_layer(layer):
                def tile(c, v, j):
                    s = v * TW + j
                    pe.wait_ge(landed[s], 16 * c + 16)
                    nc.tensor.matmul(window[v][:, 0:WIN], gathered[:, s, :], onehot[v][:, j, :],
                                     start=(j == 0), stop=(j == TW - 1)).then_inc(tiles_summed, 1)

                def iteration(t, b):
                    c = t + layer * ITERS
                    k = t * HALVES + layer * GROUPS
                    for v in range(HALVES):
                        pe.wait_ge(onehots_ready, k + v + 1)
                        pe.wait_ge(windows_added, k + v + 1)
                        for j in range(TW):
                            tile(c, v, j)
                            if b is None:
                                continue
                            if layer >= 2 and (v, j) == (0, 6):
                                turn_y(layer, b, 0)
                            if layer == 2 and (v, j) == (1, 4):
                                turn_norm(layer, b, 0)
                            if layer < GATED and (v, j) == (1, 8):
                                multiply_block(layer, b, 0)

                with pe.Fori(0, LAG) as t:
                    iteration(t, None)
                with pe.Fori(LAG, ITERS) as t:
                    iteration(t, t - LAG)
                for b, buf in zip(TAIL, TAIL_BUF):
                    tail_block(layer, b, buf)

            def unsorted_layer(layer):
                n0 = layer * ITERS * TI
                with pe.Fori(0, ITERS) as t:
                    for s in range(TI):
                        pe.wait_ge(landed[s], 16 * t + 16 * (layer * ITERS + 1))
                        for q in range(NCHUNK):
                            m = t * (TI * NCHUNK) + ((n0 + s) * NCHUNK + q)
                            pe.wait_ge(wide_ready, m + 1)
                            for a in range(4):
                                last = nc.tensor.matmul(product[:, a, 0:CW], gathered[:, s, :],
                                                        wide_onehot[:, a * CW:(a + 1) * CW], start=True, stop=True)
                            last.then_inc(wide_summed, 1)
                with pe.Fori(0, MAIN_BLOCKS) as b:
                    tail_block(layer, b, 0)
                for b, buf in zip(TAIL, TAIL_BUF):
                    tail_block(layer, b, buf)

            pe.wait_ge(check_step, 8)
            flag = pe.value_load(spread_ok[0:1, 0:1], min_val=0, max_val=1)
            with pe.If(flag > 0):
                for layer in range(LAYERS):
                    sorted_layer(layer)
            with pe.Else():
                for layer in range(LAYERS):
                    unsorted_layer(layer)


_INS = ['x', 'src', 'dst', 'edge_type_5', 'edge_type_8', 'edge_weight1', 'L0_gnn_W_in', 'L0_gnn_W_hid',
        'L0_gnn_W_out', 'L1_gnn_weight', 'L1_gnn_gate_weight', 'L1_gnn_gate_bias', 'L1_gnn_bias']


def kernel(**inputs):
    import numpy as np
    import concourse.bacc as bacc
    from concourse.bass_utils import run_bass_kernel_spmd

    nc = bacc.Bacc("TRN2", target_bir_lowering=False, num_devices=1)
    arrays, args = {}, []
    for name in _INS:
        a = np.ascontiguousarray(inputs[name])
        arrays[f"in_{name}"] = a
        args.append(nc.dram_tensor(f"in_{name}", a.shape, mybir.dt.from_np(a.dtype), kind="ExternalInput").ap())
    args.append(nc.dram_tensor("out_0", (N_NODES, D), f32, kind="ExternalOutput").ap())
    gnn_program(nc, *args)
    r = run_bass_kernel_spmd(nc, [arrays], core_ids=[0])
    return r.results[0]["out_0"]
```

```python
import concourse.bass as bass
from concourse import mybir
from contextlib import ExitStack

f32 = mybir.dt.float32
i32 = mybir.dt.int32
ALU = mybir.AluOpType
ACT = mybir.ActivationFunctionType
AX = mybir.AxisListType

P = 128
N_NODES = 6250
N_EDGES = 206250
D = 128
R0, R1 = 8, 5
SLOTS_PER_NODE = 8
LAYERS = 4
GATED = 3
TW = 13
HALVES = 2
TI = TW * HALVES
GROUP = TW * P
ITERS = -(-N_EDGES // (TI * P))
GROUPS = ITERS * HALVES
WIN = 64
BLOCK = 100
BLOCKS = -(-N_NODES // BLOCK)
NPAD = BLOCKS * BLOCK
LAST_ROWS = N_NODES - (BLOCKS - 1) * BLOCK
LAG = 2
MAIN_BLOCKS = ITERS - LAG
CHUNK = 1664
NCHUNK = 4
CW = CHUNK // 4
SUMS = CHUNK * NCHUNK
EPS = 1e-5
GCOLS = R1 * D + R1

LAST_WINDOW = N_EDGES - GROUP
REPEATED = GROUPS * GROUP - N_EDGES
LOADS = 3
LOAD_GROUPS = (GROUPS - 1) // LOADS

XBLOCKS = -(-N_NODES // P)
XLAST = N_NODES - (XBLOCKS - 1) * P
XPARTS = [(0, XLAST // 16 * 16), (XLAST // 16 * 16, XLAST)]

USES0_FIRST, USES1_FIRST = XBLOCKS // 4 + len(XPARTS), XBLOCKS // 4
TAIL = list(range(MAIN_BLOCKS, BLOCKS))
TAIL_BUF = [(i + 1) % 2 for i in range(len(TAIL))]
ENDS = list(zip(TAIL, TAIL_BUF))
USES0_LAYER = MAIN_BLOCKS + TAIL_BUF.count(0)
USES1_LAYER = TAIL_BUF.count(1)

assert SUMS >= NPAD and SUMS >= N_NODES + WIN and ITERS * TI * P - N_EDGES < GROUP
assert LOADS * LOAD_GROUPS == GROUPS - 1 and XBLOCKS % 4 == 1 and XBLOCKS // 4 == 2 + 5 * (LOADS - 1) and 0 < REPEATED < GROUP


def gnn_program(nc, x, src, dst, type5, type8, edge_w, w_in, w_hid, w_out, w_gated, gate_w, gate_b, bias, out):
    tables = [nc.dram_tensor(f"table{i}", (NPAD * SLOTS_PER_NODE, D), f32, kind="Internal").ap() for i in range(2)]
    table_rows = [t.rearrange("(n r) o -> n (r o)", r=SLOTS_PER_NODE) for t in tables]

    with ExitStack() as ctx:
        def sb(name, shape, dt=f32):
            return ctx.enter_context(nc.sbuf_tensor(name, shape, dt))

        def ps(name, shape, dt=f32):
            return ctx.enter_context(nc.psum_tensor(name, shape, dt))

        def sem(name):
            return ctx.enter_context(nc.semaphore(name))

        sums = sb("sums", [P, SUMS])
        residual = sb("residual", [P, NPAD])
        src_i = sb("src_i", [P, GROUPS, TW], i32)
        dst_i = sb("dst_i", [P, GROUPS, TW], i32)
        type_i = [sb(f"type{r}_i", [P, GROUPS, TW], i32) for r in (R0, R1)]
        row_of = [sb(f"row_of_{r}", [P, GROUPS, TW]) for r in (R0, R1)]
        weight_of = [sb("edge_weight", [P, GROUPS, TW]), sb("one_weight", [P, GROUPS, TW])]
        dst_of = sb("dst_of", [P, GROUPS, 2, TW])
        base_row = sb("base_row", [1, GROUPS], i32)
        base_all = sb("base_all", [P, GROUPS], i32)
        base_least = sb("base_least", [P, ITERS, HALVES], i32)
        base_f = sb("base_f", [P, GROUPS])
        base_least_f = sb("base_least_f", [P, GROUPS])
        src_row = sb("src_row", [P, GROUPS, TW])
        base_over = sb("base_over", [P, GROUPS])
        checks = sb("checks", [P, 6])
        bad_edges = sb("bad_edges", [P, 1])
        spread_ok = sb("spread_ok", [1, 1], i32)
        ones_col = sb("ones_col", [P, 1])
        eps_col = sb("eps_col", [P, 1])
        iota_i = sb("iota_i", [P, CHUNK], i32)
        iota_f = sb("iota_f", [P, CHUNK])
        ident = sb("ident", [P, P])
        rows_now = [sb(f"rows_now{v}", [P, TW], i32) for v in range(HALVES)]
        weight_now = [sb(f"weight_now{v}", [P, TW]) for v in range(HALVES)]
        dst_now = [sb(f"dst_now{v}", [P, 2, TW]) for v in range(HALVES)]
        gathered = sb("gathered", [P, TI, D])
        onehot = [sb(f"onehot{v}", [P, TW, WIN]) for v in range(HALVES)]
        dst_shift = sb("dst_shift", [P, NCHUNK, TW])
        wide_onehot = sb("wide_onehot", [P, CHUNK])
        weights = [sb(f"weights{i}", [P, SLOTS_PER_NODE * D]) for i in range(3)]
        weights.append(sb("weights3", [P, GCOLS]))
        bias_col = sb("bias_col", [P, 1])
        gate_b_row = sb("gate_b_row", [1, R1])
        gate_b_all = sb("gate_b_all", [P, R1])
        x_in = [sb(f"x_in{i}", [P, D]) for i in range(4)]
        h_t = [sb(f"h_t{i}", [P, P]) for i in range(2)]
        relu_t = [sb(f"relu_t{i}", [P, BLOCK]) for i in range(2)]
        y_t = [sb(f"y_t{i}", [P, BLOCK]) for i in range(2)]
        norm = [sb(f"norm{i}", [BLOCK, D]) for i in range(2)]
        stats = [sb(f"stats{i}", [BLOCK, 6]) for i in range(2)]
        mean_var = [sb(f"mean_var{i}", [BLOCK, 2]) for i in range(2)]
        std = [sb(f"std{i}", [BLOCK, 1]) for i in range(2)]
        rstd = [sb(f"rstd{i}", [BLOCK, 1]) for i in range(2)]
        logits = [sb(f"logits{i}", [BLOCK, R1]) for i in range(2)]
        gates = [sb(f"gates{i}", [BLOCK, R1]) for i in range(2)]
        rows_out = [sb(f"rows_out{i}", [P, SLOTS_PER_NODE * D]) for i in range(4)]

        window = [ps(f"window{v}", [P, 512]) for v in range(HALVES)]
        product = ps("product", [P, 4, 512])
        turned = ps("turned", [P, 512])
        turns = [turned, window[0]]
        iota_ps = ps("iota_ps", [P, 512])

        edges_loaded = [sem(f"edges_loaded{a}") for a in range(5)]
        first_loaded = sem("first_loaded")
        consts_made = sem("consts_made")
        index_step = sem("index_step")
        x_loaded = [sem(f"x_loaded{i}") for i in range(4)]
        small_loaded = sem("small_loaded")
        x_turned = sem("x_turned")
        h_ready = sem("h_ready")
        residual_cleared = sem("residual_cleared")
        residual_kept = sem("residual_kept")
        multiplied = sem("multiplied")
        rows_ready = sem("rows_ready")
        rows_stored = [sem(f"rows_stored{i}") for i in range(4)]
        check_step = sem("check_step")
        check_summed = sem("check_summed")
        iota_placed = sem("iota_placed")
        rows_staged = [sem(f"rows_staged{v}") for v in range(HALVES)]
        edges_staged = sem("edges_staged")
        landed = [sem(f"landed{s}") for s in range(TI)]
        windows_begun = sem("windows_begun")
        tiles_summed = sem("tiles_summed")
        onehots_ready = sem("onehots_ready")
        windows_added = sem("windows_added")
        sums_cleared = sem("sums_cleared")
        block_read = sem("block_read")
        relu_ready = sem("relu_ready")
        y_ready = sem("y_ready")
        y_turned = sem("y_turned")
        variance_ready = sem("variance_ready")
        rstd_ready = sem("rstd_ready")
        std_ready = sem("std_ready")
        norm_ready = sem("norm_ready")
        norm_turned = sem("norm_turned")
        logits_ready = sem("logits_ready")
        gates_ready = sem("gates_ready")
        out_stored = [sem(f"out_stored{i}") for i in range(2)]
        shifted = sem("shifted")
        wide_ready = sem("wide_ready")
        wide_summed = sem("wide_summed")
        wide_added = sem("wide_added")

        SMALL_DMAS = 13

        def block_number(layer, b):
            return XBLOCKS + BLOCKS * layer + b if layer >= 0 else b

        def norm_number(layer, b):
            return BLOCKS * (layer - 2) + b

        def buffer_uses(layer, b, buf):
            if buf == 0:
                within = b if not isinstance(b, int) or b < MAIN_BLOCKS else MAIN_BLOCKS + TAIL_BUF[:b - MAIN_BLOCKS].count(0)
                return USES0_FIRST + USES0_LAYER * layer + within
            return USES1_FIRST + USES1_LAYER * layer + TAIL_BUF[:b - MAIN_BLOCKS].count(1)

        def out_uses(b, buf):
            if buf == 0:
                return b if not isinstance(b, int) or b < MAIN_BLOCKS else MAIN_BLOCKS + TAIL_BUF[:b - MAIN_BLOCKS].count(0)
            return TAIL_BUF[:b - MAIN_BLOCKS].count(1)

        def nodes(b):
            return bass.ds(b * BLOCK, BLOCK)

        edge_arrays = [(src_i, src), (type_i[0], type8), (dst_i, dst),
                       (weight_of[0], edge_w.rearrange("e o -> (e o)")), (type_i[1], type5)]

        def edge_part(array, first, windows):
            return array[bass.ds(first, windows * GROUP)].rearrange("(g p j) -> p g j", p=P, j=TW)

        block = ctx.enter_context(nc.Block())

        @block.sync
        def _(sp):
            def load_x(b, buf, rows=P):
                sp.dma_start(x_in[buf][0:rows, :], x[bass.ds(b * P, rows), :]).then_inc(x_loaded[buf], 16)

            def store_first(b, buf, part=(0, P)):
                sp.wait_ge(rows_ready, b + 1)
                sp.dma_start(table_rows[0][bass.ds(b * P + part[0], part[1] - part[0]), :],
                             rows_out[buf][part[0]:part[1], :]).then_inc(rows_stored[buf], 16)

            def store_rows(layer, b, buf):
                sp.wait_ge(rows_ready, block_number(layer, b) + 1)
                cols = R1 * D if layer + 1 == GATED else SLOTS_PER_NODE * D
                sp.dma_start(table_rows[(layer + 1) % 2][nodes(b), 0:cols],
                             rows_out[buf][0:BLOCK, 0:cols]).then_inc(rows_stored[buf], 16)

            def store_out(b, buf, rows=BLOCK):
                sp.wait_ge(norm_ready, norm_number(GATED, b) + 1)
                sp.dma_start(out[bass.ds(b * BLOCK, rows), :], norm[buf][0:rows, :]).then_inc(out_stored[buf], 16)

            for b in range(4):
                load_x(b, b)
            sp.dma_start(weights[0][:, :].rearrange("d (r o) -> d r o", r=R0),
                         w_in.rearrange("r d o -> d r o")).then_inc(first_loaded, 16)
            with sp.Fori(0, XBLOCKS // 4 - 1) as q:
                for r in range(4):
                    sp.wait_ge(x_turned, 4 * q + r + 1)
                    load_x(4 * q + (4 + r), r)
                    store_first(4 * q + r, r)
            for b in range(XBLOCKS - 5, XBLOCKS - 1):
                if b == XBLOCKS - 5:
                    sp.wait_ge(x_turned, b + 1)
                    load_x(XBLOCKS - 1, 0, XLAST)
                store_first(b, b % 4)
            for part in XPARTS:
                store_first(XBLOCKS - 1, 0, part)

            for layer in range(LAYERS - 1):
                with sp.Fori(0, MAIN_BLOCKS) as b:
                    store_rows(layer, b, 0)
                for b, buf in ENDS:
                    store_rows(layer, b, buf)
            with sp.Fori(0, MAIN_BLOCKS) as b:
                store_out(b, 0)
            for b, buf in ENDS:
                store_out(b, buf, LAST_ROWS if b == BLOCKS - 1 else BLOCK)
            sp.wait_ge(out_stored[0], 16 * USES0_LAYER)
            sp.wait_ge(out_stored[1], 16 * USES1_LAYER)

        @block.gpsimd
        def _(pool):
            nc.gpsimd.iota(iota_i[:, :], pattern=[[1, CHUNK]], base=0, channel_multiplier=0).then_inc(consts_made, 1)
            nc.gpsimd.memset(ident[:, :], 0.0).then_inc(consts_made, 1)
            pool.wait_ge(consts_made, 2)
            nc.gpsimd.affine_select(out=ident[:, :], in_=ident[:, :], compare_op=ALU.not_equal, fill=1.0,
                                    base=0, pattern=[[-1, P]], channel_multiplier=1).then_inc(consts_made, 1)
            nc.gpsimd.tensor_copy(iota_f[:, :], iota_i[:, :]).then_inc(consts_made, 1)
            nc.gpsimd.memset(weight_of[1][:, :, :], 1.0).then_inc(consts_made, 1)
            nc.gpsimd.iota(base_least[:, :, :], pattern=[[BLOCK, ITERS], [0, HALVES]], base=-BLOCK * (LAG - 1),
                           channel_multiplier=0).then_inc(consts_made, 1)
            pool.wait_ge(consts_made, 6)
            nc.gpsimd.iota(base_least[:, ITERS - 1, HALVES - 1:HALVES], pattern=[[0, 1]],
                           base=BLOCK * (MAIN_BLOCKS + 1), channel_multiplier=0).then_inc(consts_made, 1)

            small = [0]

            def load_small(to, array):
                small[0] += 1
                pool.dma_start(to, array).then_inc(small_loaded, 16)
                pool.wait_ge(small_loaded, 16 * small[0])

            for to, array in edge_arrays:
                load_small(to[:, GROUPS - 1, :], array[LAST_WINDOW:N_EDGES].rearrange("(p j) -> p j", j=TW))
            with nc.allow_non_contiguous_dma(reason="first destination of each window, small transposed vectors"):
                load_small(base_row[0:1, 0:GROUPS - 1],
                           dst.rearrange("(o e) -> o e", o=1)[:, 0:(GROUPS - 1) * GROUP:GROUP])
                load_small(base_row[0:1, GROUPS - 1:GROUPS],
                           dst.rearrange("(o e) -> o e", o=1)[:, LAST_WINDOW:LAST_WINDOW + 1])
                load_small(gate_b_row[:, :], gate_b.rearrange("r o -> o r"))
                load_small(bias_col[:, :], bias.rearrange("(d o) -> d o", o=1))
                load_small(weights[3][:, R1 * D:GCOLS], gate_w.rearrange("r d -> d r"))
            for to, w, r in ((weights[1], w_hid, R0), (weights[2], w_out, R0), (weights[3], w_gated, R1)):
                load_small(to[:, 0:r * D].rearrange("d (r o) -> d r o", r=r), w.rearrange("r d o -> d r o"))
            assert small[0] == SMALL_DMAS
            nc.gpsimd.partition_broadcast(gate_b_all[:, :], gate_b_row[:, :]).then_inc(consts_made, 1)
            nc.gpsimd.partition_broadcast(base_all[:, :], base_row[:, :]).then_inc(index_step, 1)
            pool.wait_ge(consts_made, 8)
            nc.gpsimd.tensor_copy(base_least_f[:, :], base_least[:, :, :].rearrange("p a b -> p (a b)")
                                  ).then_inc(index_step, 1)
            pool.wait_ge(index_step, 2)
            nc.gpsimd.tensor_copy(base_f[:, :], base_all[:, :]).then_inc(index_step, 1)
            for a in range(3):
                pool.wait_ge(edges_loaded[a], 16 * LOADS)
            nc.gpsimd.tensor_scalar(src_row[:, :, :], src_i[:, :, :], float(SLOTS_PER_NODE), None,
                                    ALU.mult).then_inc(index_step, 1)
            nc.gpsimd.tensor_copy(row_of[0][:, :, :], type_i[0][:, :, :]).then_inc(index_step, 1)
            nc.gpsimd.tensor_copy(dst_of[:, :, 1, :], dst_i[:, :, :]).then_inc(index_step, 1)
            pool.wait_ge(index_step, 6)
            nc.gpsimd.tensor_tensor(row_of[0][:, :, :], row_of[0][:, :, :], src_row[:, :, :],
                                    ALU.add).then_inc(index_step, 1)
            nc.gpsimd.tensor_tensor(dst_of[:, :, 0, :], dst_of[:, :, 1, :],
                                    base_f[:, :].unsqueeze(2).to_broadcast([P, GROUPS, TW]),
                                    ALU.subtract).then_inc(index_step, 1)
            nc.gpsimd.tensor_tensor(base_over[:, :], base_f[:, :], base_least_f[:, :],
                                    ALU.subtract).then_inc(index_step, 1)
            for a in range(3, 5):
                pool.wait_ge(edges_loaded[a], 16 * LOADS)
            for w in weight_of:
                nc.gpsimd.affine_select(out=w[:, GROUPS - 1, :], in_=w[:, GROUPS - 1, :], compare_op=ALU.is_ge,
                                        fill=0.0, base=-REPEATED, pattern=[[1, TW]], channel_multiplier=TW
                                        ).then_inc(index_step, 1)
            nc.gpsimd.tensor_copy(row_of[1][:, :, :], type_i[1][:, :, :]).then_inc(index_step, 1)
            pool.wait_ge(index_step, 12)
            nc.gpsimd.tensor_tensor(row_of[1][:, :, :], row_of[1][:, :, :], src_row[:, :, :],
                                    ALU.add).then_inc(index_step, 1)

            for buf in (2, 3):
                pool.wait_ge(rows_stored[buf], 16 * (XBLOCKS // 4))
            for layer in range(LAYERS):
                pool.wait_ge(rows_stored[0], 16 * (USES0_FIRST + USES0_LAYER * layer))
                pool.wait_ge(rows_stored[1], 16 * (USES1_FIRST + USES1_LAYER * layer))
                with pool.Fori(0, ITERS) as t:
                    for v in range(HALVES):
                        pool.wait_ge(rows_staged[v], t + (layer * ITERS + 1))
                        pool.sem_inc(windows_begun, 1)
                        for j in range(TW):
                            nc.gpsimd.indirect_dma_start(
                                gathered[:, v * TW + j, :], None, tables[layer % 2][0:N_NODES * SLOTS_PER_NODE, :],
                                bass.IndirectOffsetOnAxis(ap=rows_now[v][:, j:j + 1], axis=0)
                                ).then_inc(landed[v * TW + j], 16)

        @block.scalar
        def _(act):
            def rows_from_product(layer, n, uses, buf, out_buf):
                rows = BLOCK if layer >= 0 else XLAST if isinstance(n, int) and n == XBLOCKS - 1 else P
                act.wait_ge(multiplied, n + 1)
                if uses is not None:
                    act.wait_ge(rows_stored[out_buf], 16 * uses)
                if layer + 1 == GATED:
                    act.wait_ge(logits_ready, n - (XBLOCKS + BLOCKS * layer) + 1)
                    nc.scalar.activation(gates[buf][:, :], logits[buf][:, :], ACT.Sigmoid).then_inc(gates_ready, 1)
                    act.wait_ge(gates_ready, n - (XBLOCKS + BLOCKS * layer) + 1)
                    for r in range(R1):
                        last = nc.scalar.activation(rows_out[out_buf][0:BLOCK, r * D:(r + 1) * D],
                                                    product[0:BLOCK, 2 * buf + r // 4, (r % 4) * D:(r % 4 + 1) * D],
                                                    ACT.Copy, scale=gates[buf][:, r:r + 1])
                else:
                    last = nc.scalar.activation(rows_out[out_buf][0:rows, :].rearrange("p (a b) -> p a b", a=2),
                                                product[0:rows, 2 * buf:2 * buf + 2, :], ACT.Copy)
                last.then_inc(rows_ready, 1)

            def load_edges(a, part):
                to, array = edge_arrays[a]
                act.dma_start(to[:, bass.ds(part * LOAD_GROUPS, LOAD_GROUPS), :],
                              edge_part(array, part * (LOAD_GROUPS * GROUP), LOAD_GROUPS)).then_inc(edges_loaded[a], 16)

            def first_quad(q):
                for r in range(4):
                    rows_from_product(-1, 4 * q + r, q, r % 2, r)

            for r in range(4):
                rows_from_product(-1, r, None, r % 2, r)
            for a in range(len(edge_arrays)):
                with act.Fori(0, LOADS - 1) as part:
                    load_edges(a, part)
                    first_quad(part + (1 + a * (LOADS - 1)))
                load_edges(a, LOADS - 1)
            first_quad(XBLOCKS // 4 - 1)
            rows_from_product(-1, XBLOCKS - 1, XBLOCKS // 4, 0, 0)

            def relu_block(layer, b, buf, added):
                act.wait_ge(windows_added, added)
                if layer == GATED:
                    m = norm_number(layer, b)
                    act.wait_ge(y_ready, m - 1 if isinstance(b, int) and b in TAIL else m)
                    nc.scalar.activation(relu_t[buf][:, :], sums[:, nodes(b)], ACT.Relu,
                                         bias=bias_col[:, 0:1]).then_inc(relu_ready, 1)
                else:
                    nc.scalar.activation(h_t[buf][:, 0:BLOCK], sums[:, nodes(b)], ACT.Relu).then_inc(h_ready, 1)

            def root_block(layer, b, buf):
                act.wait_ge(variance_ready, norm_number(layer, b) + 1)
                nc.scalar.activation(std[buf][:, :], mean_var[buf][:, 1:2], ACT.Sqrt,
                                     bias=eps_col[0:BLOCK, 0:1]).then_inc(std_ready, 1)

            def copy_block(layer, b, buf):
                act.wait_ge(norm_turned, norm_number(layer, b) + 1)
                nc.scalar.activation(h_t[buf][:, 0:BLOCK], turns[buf][:, P:P + BLOCK], ACT.Copy).then_inc(h_ready, 1)

            def rows_block(layer, b, buf):
                rows_from_product(layer, block_number(layer, b), buffer_uses(layer, b, buf), buf, buf)

            def turn_blocks(layer, blocks, added):
                if layer != 2:
                    for b, buf in blocks:
                        relu_block(layer, b, buf, added)
                if layer >= 2:
                    for b, buf in blocks:
                        root_block(layer, b, buf)
                if layer == 2:
                    for b, buf in blocks:
                        copy_block(layer, b, buf)
                if layer != GATED:
                    for b, buf in blocks:
                        rows_block(layer, b, buf)

            act.wait_ge(small_loaded, 16 * SMALL_DMAS)
            act.wait_ge(check_step, 1)
            for layer in range(LAYERS):
                base = 2 + layer * GROUPS
                with act.Fori(0, MAIN_BLOCKS) as b:
                    turn_blocks(layer, [(b, 0)], (b + LAG) * HALVES + base)
                turn_blocks(layer, [ENDS[0]], base + GROUPS - 1)
                turn_blocks(layer, ENDS[1:], base + GROUPS)

        @block.vector
        def _(dve):
            nc.vector.memset(residual[:, N_NODES:NPAD], 0.0).then_inc(residual_cleared, 1)
            nc.vector.memset(ones_col[:, :], 1.0).then_inc(check_step, 1)
            nc.vector.memset(eps_col[:, :], EPS)
            dve.sem_inc(windows_added, 2)

            def keep_x(n, buf, rows=P):
                dve.wait_ge(x_turned, n + 1)
                nc.vector.tensor_copy(h_t[buf][:, 0:rows], turns[buf][:, 0:rows]).then_inc(h_ready, 1)
                nc.vector.tensor_copy(residual[:, bass.ds(n * P, rows)], turns[buf][:, 0:rows]
                                      ).then_inc(residual_kept, 1)

            keep_x(0, 0)
            keep_x(1, 1)
            with dve.Fori(1, XBLOCKS // 2) as i:
                for buf in range(2):
                    dve.wait_ge(multiplied, 2 * i + buf - 1)
                    keep_x(2 * i + buf, buf)
            dve.wait_ge(multiplied, XBLOCKS - 2)
            keep_x(XBLOCKS - 1, 0, XLAST)

            def stage(layer, t, v):
                g, kind = t * HALVES + v, int(layer == GATED)
                nc.vector.tensor_copy(rows_now[v][:, :], row_of[kind][:, bass.ds(g, 1), :].rearrange("p a j -> p (a j)")
                                      ).then_inc(rows_staged[v], 1)
                nc.vector.tensor_copy(weight_now[v][:, :],
                                      weight_of[kind][:, bass.ds(g, 1), :].rearrange("p a j -> p (a j)"))
                nc.vector.tensor_copy(dst_now[v][:, :, :],
                                      dst_of[:, bass.ds(g, 1), :, :].rearrange("p a c j -> p (a c) j")
                                      ).then_inc(edges_staged, 1)

            dve.wait_ge(index_step, 13)
            for v in range(HALVES):
                stage(0, 0, v)

            dve.wait_ge(consts_made, 8)
            nc.vector.tensor_copy(iota_ps[:, 0:WIN], iota_f[:, 0:WIN]).then_inc(iota_placed, 1)
            inside = dst_of[:, :, 0, :]
            nc.vector.tensor_reduce(checks[:, 0:1], inside, AX.XY, ALU.max).then_inc(check_step, 1)
            nc.vector.tensor_reduce(checks[:, 1:2], inside, AX.XY, ALU.min).then_inc(check_step, 1)
            nc.vector.tensor_reduce(checks[:, 2:3], base_over[:, :], AX.X, ALU.min).then_inc(check_step, 1)
            dve.wait_ge(check_step, 4)
            nc.vector.tensor_scalar(checks[:, 3:4], checks[:, 0:1], float(WIN), None, ALU.is_ge).then_inc(check_step, 1)
            nc.vector.tensor_scalar(checks[:, 4:6], checks[:, 1:3], 0.0, None, ALU.is_lt).then_inc(check_step, 1)
            dve.wait_ge(check_step, 6)
            nc.vector.tensor_reduce(bad_edges[:, :], checks[:, 3:6], AX.X, ALU.add).then_inc(check_step, 1)
            dve.wait_ge(check_summed, 1)
            nc.vector.tensor_scalar(spread_ok[:, :], iota_ps[0:1, 256:257], 0.0, None, ALU.is_equal
                                    ).then_inc(check_step, 1)
            dve.wait_ge(check_step, 8)

            def read_y(layer, b, buf):
                m = norm_number(layer, b)
                if layer == GATED:
                    dve.wait_ge(relu_ready, m - BLOCKS + 1)
                    nc.vector.tensor_tensor(y_t[buf][:, :], relu_t[buf][:, :], residual[:, nodes(b)], ALU.add
                                            ).then_inc(y_ready, 1)
                else:
                    nc.vector.tensor_tensor(y_t[buf][:, :], sums[:, nodes(b)], residual[:, nodes(b)], ALU.add
                                            ).then_inc(y_ready, 1)

            def layernorm(layer, b, buf):
                m = norm_number(layer, b)
                dve.wait_ge(y_turned, m + 1)
                nc.vector.bn_stats(stats[buf][:, :], turns[buf][0:BLOCK, 0:D])
                dve.drain()
                nc.vector.bn_aggr(mean_var[buf][:, :], stats[buf][:, :]).then_inc(variance_ready, 1)
                dve.wait_ge(std_ready, m + 1)
                nc.vector.reciprocal(rstd[buf][:, :], std[buf][:, :]).then_inc(rstd_ready, 1)
                dve.wait_ge(rstd_ready, m + 1)
                if layer == GATED and not (isinstance(b, int) and out_uses(b, buf) == 0):
                    dve.wait_ge(out_stored[buf], 16 * out_uses(b, buf))
                nc.vector.tensor_scalar(norm[buf][:, :], turns[buf][0:BLOCK, 0:D], mean_var[buf][:, 0:1], rstd[buf][:, 0:1],
                                        ALU.subtract, ALU.mult).then_inc(norm_ready, 1)

            def gate_logits(layer, b, buf):
                m, n = norm_number(layer, b), block_number(layer, b)
                dve.wait_ge(multiplied, n + 1)
                nc.vector.tensor_tensor(logits[buf][:, :], product[0:BLOCK, 2 * buf + 1, D:D + R1],
                                        gate_b_all[0:BLOCK, :], ALU.add).then_inc(logits_ready, 1)
                nc.vector.tensor_copy(residual[:, nodes(b)], h_t[buf][:, 0:BLOCK]).then_inc(residual_kept, 1)

            def norm_blocks(layer, blocks):
                if layer < 2:
                    return
                for b, buf in blocks:
                    read_y(layer, b, buf)
                for b, buf in blocks:
                    layernorm(layer, b, buf)
                if layer == 2:
                    for b, buf in blocks:
                        gate_logits(layer, b, buf)

            def clear_sums(layer):
                if layer in (1, 2):
                    dve.wait_ge(h_ready, XBLOCKS + BLOCKS * layer)
                if layer == GATED:
                    dve.wait_ge(y_ready, BLOCKS)
                nc.vector.memset(sums[:, :], 0.0).then_inc(sums_cleared, 1)
                dve.wait_ge(sums_cleared, layer + 1)

            def sorted_layer(layer):
                k0 = layer * GROUPS

                def onehots(k, v):
                    dve.wait_ge(edges_staged, k + 1)
                    for j in range(TW):
                        last = nc.vector.tensor_scalar(onehot[v][:, j, :], iota_ps[:, 0:WIN], dst_now[v][:, 0, j:j + 1],
                                                       weight_now[v][:, j:j + 1], ALU.is_equal, ALU.mult)
                    last.then_inc(onehots_ready, 1)

                def add_window(t, k, v):
                    start = dve.value_load(base_row[0:1, bass.ds(t * HALVES + v, 1)], min_val=0, max_val=N_NODES - 1)
                    dve.wait_ge(tiles_summed, (k - k0) * TW + (layer * ITERS * TI + TW))
                    dve.wait_ge(windows_added, k + 2)
                    at = sums[:, bass.ds(start, WIN)]
                    nc.vector.tensor_tensor(at, at, window[v][:, 0:WIN], ALU.add).then_inc(windows_added, 1)

                def add_norm(b, buf):
                    layernorm(layer, b, buf)
                    if layer == 2:
                        gate_logits(layer, b, buf)

                def iteration(t, b, last=False):
                    k = t * HALVES + k0
                    onehots(k + 1, 1)
                    if b is not None and layer >= 2:
                        if layer == 2:
                            dve.wait_ge(windows_added, k + 2)
                        read_y(layer, b, 0)
                    add_window(t, k, 0)
                    if not last:
                        stage(layer, t + 1, 0)
                        onehots(k + 2, 0)
                    if b is not None and layer >= 2:
                        add_norm(b, 0)
                    if last and layer >= 2:
                        if layer == 2:
                            dve.wait_ge(windows_added, k + 3)
                        norm_blocks(layer, ENDS[0:1])
                    add_window(t, k + 1, 1)
                    if not last:
                        stage(layer, t + 1, 1)

                if layer > 0:
                    stage(layer, 0, 0)
                    stage(layer, 0, 1)
                onehots(k0, 0)
                clear_sums(layer)
                with dve.Fori(0, LAG) as t:
                    iteration(t, None)
                iteration(LAG, 0)
                with dve.Fori(LAG + 1, ITERS - 1) as t:
                    iteration(t, t - LAG)
                iteration(ITERS - 1, ITERS - 1 - LAG, last=True)
                if layer == 2:
                    dve.wait_ge(windows_added, 2 + k0 + GROUPS)
                norm_blocks(layer, ENDS[1:])

            def unsorted_layer(layer):
                k0, n0 = layer * GROUPS, layer * ITERS * TI
                clear_sums(layer)

                def stage_both(t):
                    for u in range(HALVES):
                        stage(layer, t, u)

                def sum_iteration(t):
                    for v in range(HALVES):
                        dve.wait_ge(edges_staged, (t + 1) * HALVES + k0)
                        for q in range(NCHUNK):
                            last = nc.vector.tensor_scalar(dst_shift[:, q, :], dst_now[v][:, 1, :], float(-q * CHUNK),
                                                           None, ALU.add)
                        last.then_inc(shifted, 1)
                        dve.wait_ge(shifted, t * HALVES + (k0 + v + 1))
                        for j in range(TW):
                            for q in range(NCHUNK):
                                m = t * (TI * NCHUNK) + ((n0 + v * TW + j) * NCHUNK + q)
                                nc.vector.tensor_scalar(wide_onehot[:, :], iota_f[:, :], dst_shift[:, q, j:j + 1],
                                                        weight_now[v][:, j:j + 1], ALU.is_equal, ALU.mult
                                                        ).then_inc(wide_ready, 1)
                                dve.wait_ge(wide_summed, m + 1)
                                at = sums[:, q * CHUNK:(q + 1) * CHUNK].rearrange("p (a b) -> p a b", a=4)
                                nc.vector.tensor_tensor(at, at, product[:, :, 0:CW], ALU.add).then_inc(wide_added, 1)

                if layer > 0:
                    stage_both(0)
                sum_iteration(0)
                with dve.Fori(1, ITERS) as t:
                    stage_both(t)
                    sum_iteration(t)
                dve.wait_ge(wide_added, (layer + 1) * ITERS * TI * NCHUNK)
                dve.sem_inc(windows_added, GROUPS)
                if layer >= 2:
                    norm_blocks(layer, [(0, 0)])
                    with dve.Fori(1, MAIN_BLOCKS) as b:
                        norm_blocks(layer, [(b, 0)])
                norm_blocks(layer, ENDS[0:1])
                norm_blocks(layer, ENDS[1:])

            flag = dve.value_load(spread_ok[0:1, 0:1], min_val=0, max_val=1)
            with dve.If(flag > 0):
                for layer in range(LAYERS):
                    sorted_layer(layer)
            with dve.Else():
                for layer in range(LAYERS):
                    unsorted_layer(layer)

        @block.tensor
        def _(pe):
            def turn_x(n, buf, x_buf, uses, rows=P):
                pe.wait_ge(x_loaded[x_buf], 16 * (uses + 1))
                nc.tensor.transpose(turns[buf][:, 0:rows], x_in[x_buf][0:rows, :],
                                    ident[0:rows, 0:rows]).then_inc(x_turned, 1)

            def multiply(layer, n, buf, rows=BLOCK):
                pe.wait_ge(h_ready, n + 1)
                w = weights[layer + 1]
                cols = GCOLS if layer + 1 == GATED else SLOTS_PER_NODE * D
                nc.tensor.matmul(product[0:rows, 2 * buf, :], h_t[buf][:, 0:rows], w[:, 0:512], start=True, stop=True)
                nc.tensor.matmul(product[0:rows, 2 * buf + 1, 0:cols - 512], h_t[buf][:, 0:rows], w[:, 512:cols],
                                 start=True, stop=True).then_inc(multiplied, 1)

            pe.wait_ge(consts_made, 3)
            turn_x(0, 0, 0, 0)
            turn_x(1, 1, 1, 0)
            pe.wait_ge(first_loaded, 16)
            multiply(-1, 0, 0, P)
            multiply(-1, 1, 1, P)

            def first_pair(n, x_buf, uses):
                for buf in range(2):
                    pe.wait_ge(residual_kept, n + (buf - 1))
                    turn_x(n + buf, buf, x_buf + buf, uses)
                for buf in range(2):
                    pe.wait_ge(rows_ready, n + (buf - 1))
                    multiply(-1, n + buf, buf, P)

            first_pair(2, 2, 0)
            with pe.Fori(1, XBLOCKS // 4) as q:
                first_pair(4 * q, 0, q)
                first_pair(4 * q + 2, 2, q)
            pe.wait_ge(residual_kept, XBLOCKS - 2)
            turn_x(XBLOCKS - 1, 0, 0, XBLOCKS // 4, XLAST)
            pe.wait_ge(rows_ready, XBLOCKS - 2)
            multiply(-1, XBLOCKS - 1, 0, XLAST)

            pe.wait_ge(small_loaded, 16 * SMALL_DMAS)
            pe.wait_ge(check_step, 7)
            nc.tensor.matmul(iota_ps[0:1, 256:257], bad_edges[:, :], ones_col[:, :], start=True, stop=True
                             ).then_inc(check_summed, 1)

            def turn_y(layer, b, buf):
                m = norm_number(layer, b)
                pe.wait_ge(y_ready, m + 1)
                nc.tensor.transpose(turns[buf][0:BLOCK, 0:D], y_t[buf][:, :], ident[:, :]).then_inc(y_turned, 1)

            def turn_norm(layer, b, buf):
                m = norm_number(layer, b)
                pe.wait_ge(norm_ready, m + 1)
                nc.tensor.transpose(turns[buf][:, P:P + BLOCK], norm[buf][:, :], ident[0:BLOCK, 0:BLOCK]
                                    ).then_inc(norm_turned, 1)

            def multiply_block(layer, b, buf):
                n = block_number(layer, b)
                pe.wait_ge(rows_ready, n - 1 if isinstance(b, int) and b in TAIL else n)
                multiply(layer, n, buf)

            def turn_blocks(layer, blocks):
                if layer >= 2:
                    for b, buf in blocks:
                        turn_y(layer, b, buf)
                if layer == 2:
                    for b, buf in blocks:
                        turn_norm(layer, b, buf)
                if layer < GATED:
                    for b, buf in blocks:
                        multiply_block(layer, b, buf)

            def sorted_layer(layer):
                def tile(c, v, j):
                    s = v * TW + j
                    pe.wait_ge(landed[s], 16 * c + 16)
                    nc.tensor.matmul(window[v][:, 0:WIN], gathered[:, s, :], onehot[v][:, j, :],
                                     start=(j == 0), stop=(j == TW - 1)).then_inc(tiles_summed, 1)

                def iteration(t, b, last=False):
                    c = t + layer * ITERS
                    k = t * HALVES + layer * GROUPS
                    for v in range(HALVES):
                        pe.wait_ge(onehots_ready, k + v + 1)
                        pe.wait_ge(windows_added, k + v + 1)
                        for j in range(TW):
                            tile(c, v, j)
                            if b is None:
                                continue
                            if layer >= 2 and (v, j) == (0, 6):
                                turn_y(layer, b, 0)
                            if layer == 2 and (v, j) == (1, 2 if last else 4):
                                turn_norm(layer, b, 0)
                            if layer < GATED and (v, j) == (1, 4 if last else 8):
                                multiply_block(layer, b, 0)
                            if last and layer >= 2 and (v, j) == (1, 6):
                                turn_y(layer, *ENDS[0])
                            if last and layer == 2 and (v, j) == (1, 8):
                                turn_norm(layer, *ENDS[0])
                            if last and layer < GATED and (v, j) == (1, 10):
                                multiply_block(layer, *ENDS[0])

                with pe.Fori(0, LAG) as t:
                    iteration(t, None)
                with pe.Fori(LAG, ITERS - 1) as t:
                    iteration(t, t - LAG)
                iteration(ITERS - 1, ITERS - 1 - LAG, last=True)
                turn_blocks(layer, ENDS[1:])

            def unsorted_layer(layer):
                n0 = layer * ITERS * TI
                with pe.Fori(0, ITERS) as t:
                    for s in range(TI):
                        pe.wait_ge(landed[s], 16 * t + 16 * (layer * ITERS + 1))
                        for q in range(NCHUNK):
                            m = t * (TI * NCHUNK) + ((n0 + s) * NCHUNK + q)
                            pe.wait_ge(wide_ready, m + 1)
                            for a in range(4):
                                last = nc.tensor.matmul(product[:, a, 0:CW], gathered[:, s, :],
                                                        wide_onehot[:, a * CW:(a + 1) * CW], start=True, stop=True)
                            last.then_inc(wide_summed, 1)
                with pe.Fori(0, MAIN_BLOCKS) as b:
                    turn_blocks(layer, [(b, 0)])
                turn_blocks(layer, ENDS[0:1])
                turn_blocks(layer, ENDS[1:])

            pe.wait_ge(check_step, 8)
            flag = pe.value_load(spread_ok[0:1, 0:1], min_val=0, max_val=1)
            with pe.If(flag > 0):
                for layer in range(LAYERS):
                    sorted_layer(layer)
            with pe.Else():
                for layer in range(LAYERS):
                    unsorted_layer(layer)


_INS = ['x', 'src', 'dst', 'edge_type_5', 'edge_type_8', 'edge_weight1', 'L0_gnn_W_in', 'L0_gnn_W_hid',
        'L0_gnn_W_out', 'L1_gnn_weight', 'L1_gnn_gate_weight', 'L1_gnn_gate_bias', 'L1_gnn_bias']


def kernel(**inputs):
    import numpy as np
    import concourse.bacc as bacc
    from concourse.bass_utils import run_bass_kernel_spmd

    nc = bacc.Bacc("TRN2", target_bir_lowering=False, num_devices=1)
    arrays, args = {}, []
    for name in _INS:
        a = np.ascontiguousarray(inputs[name])
        arrays[f"in_{name}"] = a
        args.append(nc.dram_tensor(f"in_{name}", a.shape, mybir.dt.from_np(a.dtype), kind="ExternalInput").ap())
    args.append(nc.dram_tensor("out_0", (N_NODES, D), f32, kind="ExternalOutput").ap())
    gnn_program(nc, *args)
    r = run_bass_kernel_spmd(nc, [arrays], core_ids=[0])
    return r.results[0]["out_0"]
```

```python
import concourse.bass as bass
from concourse import mybir
from contextlib import ExitStack

f32 = mybir.dt.float32
i32 = mybir.dt.int32
ALU = mybir.AluOpType
ACT = mybir.ActivationFunctionType
AX = mybir.AxisListType

P = 128
N_NODES = 6250
N_EDGES = 206250
D = 128
R0, R1 = 8, 5
SLOTS_PER_NODE = 8
LAYERS = 4
GATED = 3
TW = 13
HALVES = 2
TI = TW * HALVES
GROUP = TW * P
ITERS = -(-N_EDGES // (TI * P))
GROUPS = ITERS * HALVES
WIN = 64
BLOCK = 100
BLOCKS = -(-N_NODES // BLOCK)
NPAD = BLOCKS * BLOCK
LAST_ROWS = N_NODES - (BLOCKS - 1) * BLOCK
LAG = 2
MAIN_BLOCKS = ITERS - LAG
CHUNK = 1664
NCHUNK = 4
CW = CHUNK // 4
SUMS = CHUNK * NCHUNK
EPS = 1e-5
GCOLS = R1 * D + R1

LAST_WINDOW = N_EDGES - GROUP
REPEATED = GROUPS * GROUP - N_EDGES
LOADS = 3
LOAD_GROUPS = (GROUPS - 1) // LOADS

XBLOCKS = -(-N_NODES // P)
XLAST = N_NODES - (XBLOCKS - 1) * P
XPARTS = [(0, XLAST // 16 * 16), (XLAST // 16 * 16, XLAST)]

USES0_FIRST, USES1_FIRST = XBLOCKS // 4 + len(XPARTS), XBLOCKS // 4
TAIL = list(range(MAIN_BLOCKS, BLOCKS))
TAIL_BUF = [(i + 1) % 2 for i in range(len(TAIL))]
ENDS = list(zip(TAIL, TAIL_BUF))
USES0_LAYER = MAIN_BLOCKS + TAIL_BUF.count(0)
USES1_LAYER = TAIL_BUF.count(1)

assert SUMS >= NPAD and SUMS >= N_NODES + WIN and ITERS * TI * P - N_EDGES < GROUP
assert LOADS * LOAD_GROUPS == GROUPS - 1 and XBLOCKS % 4 == 1 and XBLOCKS // 4 > 1 + 2 * LOADS and 0 < REPEATED < GROUP


def gnn_program(nc, x, src, dst, type5, type8, edge_w, w_in, w_hid, w_out, w_gated, gate_w, gate_b, bias, out):
    tables = [nc.dram_tensor(f"table{i}", (NPAD * SLOTS_PER_NODE, D), f32, kind="Internal").ap() for i in range(2)]
    table_rows = [t.rearrange("(n r) o -> n (r o)", r=SLOTS_PER_NODE) for t in tables]

    with ExitStack() as ctx:
        def sb(name, shape, dt=f32):
            return ctx.enter_context(nc.sbuf_tensor(name, shape, dt))

        def ps(name, shape, dt=f32):
            return ctx.enter_context(nc.psum_tensor(name, shape, dt))

        def sem(name):
            return ctx.enter_context(nc.semaphore(name))

        sums = sb("sums", [P, SUMS])
        residual = sb("residual", [P, NPAD])
        src_i = sb("src_i", [P, GROUPS, TW], i32)
        dst_i = sb("dst_i", [P, GROUPS, TW], i32)
        type_i = [sb(f"type{r}_i", [P, GROUPS, TW], i32) for r in (R0, R1)]
        row_of = [sb(f"row_of_{r}", [P, GROUPS, TW]) for r in (R0, R1)]
        weight_of = [sb("edge_weight", [P, GROUPS, TW]), sb("one_weight", [P, GROUPS, TW])]
        dst_of = sb("dst_of", [P, GROUPS, 2, TW])
        base_row = sb("base_row", [1, GROUPS], i32)
        base_all = sb("base_all", [P, GROUPS], i32)
        base_least = sb("base_least", [P, ITERS, HALVES], i32)
        base_f = sb("base_f", [P, GROUPS])
        base_least_f = sb("base_least_f", [P, GROUPS])
        src_row = sb("src_row", [P, GROUPS, TW])
        base_over = sb("base_over", [P, GROUPS])
        checks = sb("checks", [P, 6])
        bad_edges = sb("bad_edges", [P, 1])
        spread_ok = sb("spread_ok", [1, 1], i32)
        ones_col = sb("ones_col", [P, 1])
        eps_col = sb("eps_col", [P, 1])
        iota_i = sb("iota_i", [P, CHUNK], i32)
        iota_f = sb("iota_f", [P, CHUNK])
        ident = sb("ident", [P, P])
        rows_now = [sb(f"rows_now{v}", [P, TW], i32) for v in range(HALVES)]
        weight_now = [sb(f"weight_now{v}", [P, TW]) for v in range(HALVES)]
        dst_now = [sb(f"dst_now{v}", [P, 2, TW]) for v in range(HALVES)]
        gathered = sb("gathered", [P, TI, D])
        onehot = [sb(f"onehot{v}", [P, TW, WIN]) for v in range(HALVES)]
        dst_shift = sb("dst_shift", [P, NCHUNK, TW])
        wide_onehot = sb("wide_onehot", [P, CHUNK])
        weights = [sb(f"weights{i}", [P, SLOTS_PER_NODE * D]) for i in range(3)]
        weights.append(sb("weights3", [P, GCOLS]))
        bias_col = sb("bias_col", [P, 1])
        gate_b_row = sb("gate_b_row", [1, R1])
        gate_b_all = sb("gate_b_all", [P, R1])
        x_in = [sb(f"x_in{i}", [P, D]) for i in range(4)]
        h_t = [sb(f"h_t{i}", [P, P]) for i in range(2)]
        relu_t = [sb(f"relu_t{i}", [P, BLOCK]) for i in range(2)]
        y_t = [sb(f"y_t{i}", [P, BLOCK]) for i in range(2)]
        norm = [sb(f"norm{i}", [BLOCK, D]) for i in range(2)]
        stats = [sb(f"stats{i}", [BLOCK, 6]) for i in range(2)]
        mean_var = [sb(f"mean_var{i}", [BLOCK, 2]) for i in range(2)]
        std = [sb(f"std{i}", [BLOCK, 1]) for i in range(2)]
        rstd = [sb(f"rstd{i}", [BLOCK, 1]) for i in range(2)]
        logits = [sb(f"logits{i}", [BLOCK, R1]) for i in range(2)]
        gates = [sb(f"gates{i}", [BLOCK, R1]) for i in range(2)]
        rows_out = [sb(f"rows_out{i}", [P, SLOTS_PER_NODE * D]) for i in range(4)]

        window = [ps(f"window{v}", [P, 512]) for v in range(HALVES)]
        product = ps("product", [P, 4, 512])
        turned = ps("turned", [P, 512])
        turns = [turned, window[0]]
        iota_ps = ps("iota_ps", [P, 512])

        edges_loaded = [sem(f"edges_loaded{a}") for a in range(5)]
        first_loaded = sem("first_loaded")
        consts_made = sem("consts_made")
        index_step = sem("index_step")
        dst_step = sem("dst_step")
        gated_row_step = sem("gated_row_step")
        x_loaded = [sem(f"x_loaded{i}") for i in range(4)]
        small_loaded = sem("small_loaded")
        weights_loaded = sem("weights_loaded")
        x_turned = sem("x_turned")
        h_ready = sem("h_ready")
        residual_cleared = sem("residual_cleared")
        residual_kept = sem("residual_kept")
        multiplied = sem("multiplied")
        rows_ready = sem("rows_ready")
        rows_stored = [sem(f"rows_stored{i}") for i in range(4)]
        check_step = sem("check_step")
        check_summed = sem("check_summed")
        iota_placed = sem("iota_placed")
        rows_staged = [sem(f"rows_staged{v}") for v in range(HALVES)]
        edges_staged = sem("edges_staged")
        landed = [sem(f"landed{s}") for s in range(TI)]
        windows_begun = sem("windows_begun")
        tiles_summed = sem("tiles_summed")
        onehots_ready = sem("onehots_ready")
        windows_added = sem("windows_added")
        sums_cleared = sem("sums_cleared")
        relu_ready = sem("relu_ready")
        y_ready = sem("y_ready")
        y_turned = sem("y_turned")
        variance_ready = sem("variance_ready")
        rstd_ready = sem("rstd_ready")
        std_ready = sem("std_ready")
        norm_ready = sem("norm_ready")
        norm_turned = sem("norm_turned")
        logits_ready = sem("logits_ready")
        gates_ready = sem("gates_ready")
        out_stored = [sem(f"out_stored{i}") for i in range(2)]
        shifted = sem("shifted")
        wide_ready = sem("wide_ready")
        wide_summed = sem("wide_summed")
        wide_added = sem("wide_added")

        SMALL_DMAS = 10

        def block_number(layer, b):
            return XBLOCKS + BLOCKS * layer + b if layer >= 0 else b

        def norm_number(layer, b):
            return BLOCKS * (layer - 2) + b

        def buffer_uses(layer, b, buf):
            if buf == 0:
                within = b if not isinstance(b, int) or b < MAIN_BLOCKS else MAIN_BLOCKS + TAIL_BUF[:b - MAIN_BLOCKS].count(0)
                return USES0_FIRST + USES0_LAYER * layer + within
            return USES1_FIRST + USES1_LAYER * layer + TAIL_BUF[:b - MAIN_BLOCKS].count(1)

        def out_uses(b, buf):
            if buf == 0:
                return b if not isinstance(b, int) or b < MAIN_BLOCKS else MAIN_BLOCKS + TAIL_BUF[:b - MAIN_BLOCKS].count(0)
            return TAIL_BUF[:b - MAIN_BLOCKS].count(1)

        def nodes(b):
            return bass.ds(b * BLOCK, BLOCK)

        edge_arrays = [(src_i, src), (type_i[0], type8), (dst_i, dst),
                       (weight_of[0], edge_w.rearrange("e o -> (e o)")), (type_i[1], type5)]

        def edge_part(array, first, windows):
            return array[bass.ds(first, windows * GROUP)].rearrange("(g p j) -> p g j", p=P, j=TW)

        block = ctx.enter_context(nc.Block())

        @block.sync
        def _(sp):
            def load_x(b, buf, rows=P):
                sp.dma_start(x_in[buf][0:rows, :], x[bass.ds(b * P, rows), :]).then_inc(x_loaded[buf], 16)

            def store_first(b, buf, part=(0, P)):
                sp.wait_ge(rows_ready, b + 1)
                sp.dma_start(table_rows[0][bass.ds(b * P + part[0], part[1] - part[0]), :],
                             rows_out[buf][part[0]:part[1], :]).then_inc(rows_stored[buf], 16)

            def store_rows(layer, b, buf):
                sp.wait_ge(rows_ready, block_number(layer, b) + 1)
                cols = R1 * D if layer + 1 == GATED else SLOTS_PER_NODE * D
                sp.dma_start(table_rows[(layer + 1) % 2][nodes(b), 0:cols],
                             rows_out[buf][0:BLOCK, 0:cols]).then_inc(rows_stored[buf], 16)

            def store_out(b, buf, rows=BLOCK):
                sp.wait_ge(norm_ready, norm_number(GATED, b) + 1)
                sp.dma_start(out[bass.ds(b * BLOCK, rows), :], norm[buf][0:rows, :]).then_inc(out_stored[buf], 16)

            for b in range(4):
                load_x(b, b)
            sp.dma_start(weights[0][:, :].rearrange("d (r o) -> d r o", r=R0),
                         w_in.rearrange("r d o -> d r o")).then_inc(first_loaded, 16)
            for b in range(4, 6):
                sp.wait_ge(x_turned, b - 3)
                load_x(b, b - 4)
            with sp.Fori(0, XBLOCKS // 4 - 2) as q:
                for r in range(4):
                    sp.wait_ge(x_turned, 4 * q + r + 3)
                    load_x(4 * q + (6 + r), (r + 2) % 4)
                    store_first(4 * q + r, r)
            for b in range(XBLOCKS - 9, XBLOCKS - 1):
                if b + 6 < XBLOCKS:
                    sp.wait_ge(x_turned, b + 3)
                    load_x(b + 6, (b + 2) % 4, P if b + 7 < XBLOCKS else XLAST)
                store_first(b, b % 4)
            for part in XPARTS:
                store_first(XBLOCKS - 1, 0, part)
            sp.wait_ge(edges_loaded[3], 16 * LOADS)
            for to, w, r in ((weights[1], w_hid, R0), (weights[2], w_out, R0), (weights[3], w_gated, R1)):
                sp.dma_start(to[:, 0:r * D].rearrange("d (r o) -> d r o", r=r),
                             w.rearrange("r d o -> d r o")).then_inc(weights_loaded, 16)

            for layer in range(LAYERS - 1):
                with sp.Fori(0, MAIN_BLOCKS) as b:
                    store_rows(layer, b, 0)
                for b, buf in ENDS:
                    store_rows(layer, b, buf)
            with sp.Fori(0, MAIN_BLOCKS) as b:
                store_out(b, 0)
            for b, buf in ENDS:
                store_out(b, buf, LAST_ROWS if b == BLOCKS - 1 else BLOCK)
            sp.wait_ge(out_stored[0], 16 * USES0_LAYER)
            sp.wait_ge(out_stored[1], 16 * USES1_LAYER)

        @block.gpsimd
        def _(pool):
            nc.gpsimd.iota(iota_i[:, :], pattern=[[1, CHUNK]], base=0, channel_multiplier=0).then_inc(consts_made, 1)
            nc.gpsimd.memset(ident[:, :], 0.0).then_inc(consts_made, 1)
            pool.wait_ge(consts_made, 2)
            nc.gpsimd.affine_select(out=ident[:, :], in_=ident[:, :], compare_op=ALU.not_equal, fill=1.0,
                                    base=0, pattern=[[-1, P]], channel_multiplier=1).then_inc(consts_made, 1)
            nc.gpsimd.tensor_copy(iota_f[:, :], iota_i[:, :]).then_inc(consts_made, 1)
            nc.gpsimd.memset(weight_of[1][:, :, :], 1.0).then_inc(consts_made, 1)
            nc.gpsimd.iota(base_least[:, :, :], pattern=[[BLOCK, ITERS], [0, HALVES]], base=-BLOCK * (LAG - 1),
                           channel_multiplier=0).then_inc(consts_made, 1)
            pool.wait_ge(consts_made, 6)
            nc.gpsimd.iota(base_least[:, ITERS - 1, HALVES - 1:HALVES], pattern=[[0, 1]],
                           base=BLOCK * (MAIN_BLOCKS + 1), channel_multiplier=0).then_inc(consts_made, 1)

            small = [0]

            def load_small(to, array):
                small[0] += 1
                pool.dma_start(to, array).then_inc(small_loaded, 16)

            def wait_small():
                pool.wait_ge(small_loaded, 16 * small[0])

            for to, array in edge_arrays:
                load_small(to[:, GROUPS - 1, :], array[LAST_WINDOW:N_EDGES].rearrange("(p j) -> p j", j=TW))
                wait_small()
            with nc.allow_non_contiguous_dma(reason="first destination of each window"):
                load_small(base_row[0:1, 0:GROUPS - 1],
                           dst.rearrange("(o e) -> o e", o=1)[:, 0:(GROUPS - 1) * GROUP:GROUP])
                wait_small()
                load_small(base_row[0:1, GROUPS - 1:GROUPS],
                           dst.rearrange("(o e) -> o e", o=1)[:, LAST_WINDOW:LAST_WINDOW + 1])
                wait_small()
            nc.gpsimd.partition_broadcast(base_all[:, :], base_row[:, :]).then_inc(index_step, 1)
            pool.wait_ge(consts_made, 7)
            nc.gpsimd.tensor_copy(base_least_f[:, :], base_least[:, :, :].rearrange("p a b -> p (a b)")
                                  ).then_inc(index_step, 1)
            pool.wait_ge(index_step, 2)
            nc.gpsimd.tensor_copy(base_f[:, :], base_all[:, :]).then_inc(index_step, 1)

            with nc.allow_non_contiguous_dma(reason="small transposed vectors"):
                load_small(gate_b_row[:, :], gate_b.rearrange("r o -> o r"))
                pool.wait_ge(edges_loaded[0], 16 * LOADS)
                nc.gpsimd.tensor_scalar(src_row[:, :, :], src_i[:, :, :], float(SLOTS_PER_NODE), None,
                                        ALU.mult).then_inc(index_step, 1)
                wait_small()
                nc.gpsimd.partition_broadcast(gate_b_all[:, :], gate_b_row[:, :]).then_inc(consts_made, 1)
                load_small(bias_col[:, :], bias.rearrange("(d o) -> d o", o=1))
                pool.wait_ge(edges_loaded[1], 16 * LOADS)
                nc.gpsimd.tensor_copy(row_of[0][:, :, :], type_i[0][:, :, :]).then_inc(index_step, 1)
                wait_small()
                load_small(weights[3][:, R1 * D:GCOLS], gate_w.rearrange("r d -> d r"))
                pool.wait_ge(index_step, 5)
                nc.gpsimd.tensor_tensor(row_of[0][:, :, :], row_of[0][:, :, :], src_row[:, :, :],
                                        ALU.add).then_inc(index_step, 1)
                wait_small()
            assert small[0] == SMALL_DMAS
            nc.gpsimd.tensor_tensor(base_over[:, :], base_f[:, :], base_least_f[:, :],
                                    ALU.subtract).then_inc(index_step, 1)
            for w in weight_of:
                nc.gpsimd.affine_select(out=w[:, GROUPS - 1, :], in_=w[:, GROUPS - 1, :], compare_op=ALU.is_ge,
                                        fill=0.0, base=-REPEATED, pattern=[[1, TW]], channel_multiplier=TW
                                        ).then_inc(index_step, 1)

            for buf in (2, 3):
                pool.wait_ge(rows_stored[buf], 16 * (XBLOCKS // 4))
            for layer in range(LAYERS):
                pool.wait_ge(rows_stored[0], 16 * (USES0_FIRST + USES0_LAYER * layer))
                pool.wait_ge(rows_stored[1], 16 * (USES1_FIRST + USES1_LAYER * layer))
                with pool.Fori(0, ITERS) as t:
                    for v in range(HALVES):
                        pool.wait_ge(rows_staged[v], t + (layer * ITERS + 1))
                        pool.sem_inc(windows_begun, 1)
                        for j in range(TW):
                            nc.gpsimd.indirect_dma_start(
                                gathered[:, v * TW + j, :], None, tables[layer % 2][0:N_NODES * SLOTS_PER_NODE, :],
                                bass.IndirectOffsetOnAxis(ap=rows_now[v][:, j:j + 1], axis=0)
                                ).then_inc(landed[v * TW + j], 16)

        @block.scalar
        def _(act):
            def rows_from_product(layer, n, uses, buf, out_buf):
                rows = BLOCK if layer >= 0 else XLAST if isinstance(n, int) and n == XBLOCKS - 1 else P
                act.wait_ge(multiplied, n + 1)
                if uses is not None:
                    act.wait_ge(rows_stored[out_buf], 16 * uses)
                if layer + 1 == GATED:
                    act.wait_ge(logits_ready, n - (XBLOCKS + BLOCKS * layer) + 1)
                    nc.scalar.activation(gates[buf][:, :], logits[buf][:, :], ACT.Sigmoid).then_inc(gates_ready, 1)
                    act.wait_ge(gates_ready, n - (XBLOCKS + BLOCKS * layer) + 1)
                    for r in range(R1):
                        last = nc.scalar.activation(rows_out[out_buf][0:BLOCK, r * D:(r + 1) * D],
                                                    product[0:BLOCK, 2 * buf + r // 4, (r % 4) * D:(r % 4 + 1) * D],
                                                    ACT.Copy, scale=gates[buf][:, r:r + 1])
                else:
                    last = nc.scalar.activation(rows_out[out_buf][0:rows, :].rearrange("p (a b) -> p a b", a=2),
                                                product[0:rows, 2 * buf:2 * buf + 2, :], ACT.Copy)
                last.then_inc(rows_ready, 1)

            def load_edges(a, part):
                to, array = edge_arrays[a]
                act.dma_start(to[:, bass.ds(part * LOAD_GROUPS, LOAD_GROUPS), :],
                              edge_part(array, part * (LOAD_GROUPS * GROUP), LOAD_GROUPS)).then_inc(edges_loaded[a], 16)

            def first_quad(q):
                for r in range(4):
                    rows_from_product(-1, 4 * q + r, q, r % 2, r)

            for r in range(4):
                rows_from_product(-1, r, None, r % 2, r)
            for a in range(2):
                with act.Fori(0, LOADS) as part:
                    load_edges(a, part)
                    first_quad(part + (1 + a * LOADS))
            with act.Fori(1 + 2 * LOADS, XBLOCKS // 4) as q:
                first_quad(q)
            rows_from_product(-1, XBLOCKS - 1, XBLOCKS // 4, 0, 0)
            act.wait_ge(rows_stored[0], 16 * USES0_FIRST)
            for a in range(2, len(edge_arrays)):
                for part in range(LOADS):
                    load_edges(a, part)

            def relu_block(layer, b, buf, added):
                act.wait_ge(windows_added, added)
                if layer == GATED:
                    m = norm_number(layer, b)
                    act.wait_ge(y_ready, m - 1 if isinstance(b, int) and b in TAIL else m)
                    nc.scalar.activation(relu_t[buf][:, :], sums[:, nodes(b)], ACT.Relu,
                                         bias=bias_col[:, 0:1]).then_inc(relu_ready, 1)
                else:
                    nc.scalar.activation(h_t[buf][:, 0:BLOCK], sums[:, nodes(b)], ACT.Relu).then_inc(h_ready, 1)

            def root_block(layer, b, buf):
                act.wait_ge(variance_ready, norm_number(layer, b) + 1)
                nc.scalar.activation(std[buf][:, :], mean_var[buf][:, 1:2], ACT.Sqrt,
                                     bias=eps_col[0:BLOCK, 0:1]).then_inc(std_ready, 1)

            def copy_block(layer, b, buf):
                act.wait_ge(norm_turned, norm_number(layer, b) + 1)
                nc.scalar.activation(h_t[buf][:, 0:BLOCK], turns[buf][:, P:P + BLOCK], ACT.Copy).then_inc(h_ready, 1)

            def rows_block(layer, b, buf):
                rows_from_product(layer, block_number(layer, b), buffer_uses(layer, b, buf), buf, buf)

            def turn_blocks(layer, blocks, added):
                if layer != 2:
                    for b, buf in blocks:
                        relu_block(layer, b, buf, added)
                if layer >= 2:
                    for b, buf in blocks:
                        root_block(layer, b, buf)
                if layer == 2:
                    for b, buf in blocks:
                        copy_block(layer, b, buf)
                if layer != GATED:
                    for b, buf in blocks:
                        rows_block(layer, b, buf)

            act.wait_ge(small_loaded, 16 * SMALL_DMAS)
            act.wait_ge(check_step, 1)
            for layer in range(LAYERS):
                base = 2 + layer * GROUPS
                with act.Fori(0, MAIN_BLOCKS) as b:
                    turn_blocks(layer, [(b, 0)], (b + LAG) * HALVES + base)
                turn_blocks(layer, [ENDS[0]], base + GROUPS - 1)
                turn_blocks(layer, ENDS[1:], base + GROUPS)

        @block.vector
        def _(dve):
            nc.vector.memset(residual[:, N_NODES:NPAD], 0.0).then_inc(residual_cleared, 1)
            nc.vector.memset(ones_col[:, :], 1.0).then_inc(check_step, 1)
            nc.vector.memset(eps_col[:, :], EPS)
            dve.sem_inc(windows_added, 2)

            def keep_x(n, buf, rows=P):
                dve.wait_ge(x_turned, n + 1)
                nc.vector.tensor_copy(h_t[buf][:, 0:rows], turns[buf][:, 0:rows]).then_inc(h_ready, 1)
                nc.vector.tensor_copy(residual[:, bass.ds(n * P, rows)], turns[buf][:, 0:rows]
                                      ).then_inc(residual_kept, 1)

            keep_x(0, 0)
            keep_x(1, 1)
            with dve.Fori(1, XBLOCKS // 2) as i:
                for buf in range(2):
                    dve.wait_ge(multiplied, 2 * i + buf - 1)
                    keep_x(2 * i + buf, buf)
            dve.wait_ge(multiplied, XBLOCKS - 2)
            keep_x(XBLOCKS - 1, 0, XLAST)

            def stage_rows(layer, t, v):
                nc.vector.tensor_copy(rows_now[v][:, :], row_of[int(layer == GATED)][:, bass.ds(t * HALVES + v, 1), :]
                                      .rearrange("p a j -> p (a j)")).then_inc(rows_staged[v], 1)

            def stage_edges(layer, t, v):
                g = t * HALVES + v
                nc.vector.tensor_copy(weight_now[v][:, :], weight_of[int(layer == GATED)][:, bass.ds(g, 1), :]
                                      .rearrange("p a j -> p (a j)"))
                nc.vector.tensor_copy(dst_now[v][:, :, :],
                                      dst_of[:, bass.ds(g, 1), :, :].rearrange("p a c j -> p (a c) j")
                                      ).then_inc(edges_staged, 1)

            def stage(layer, t, v):
                stage_rows(layer, t, v)
                stage_edges(layer, t, v)

            dve.wait_ge(index_step, 9)
            for v in range(HALVES):
                stage_rows(0, 0, v)

            def clear_sums(layer):
                if layer in (1, 2):
                    dve.wait_ge(h_ready, XBLOCKS + BLOCKS * layer)
                if layer == GATED:
                    dve.wait_ge(y_ready, BLOCKS)
                nc.vector.memset(sums[:, :], 0.0).then_inc(sums_cleared, 1)
                dve.wait_ge(sums_cleared, layer + 1)

            clear_sums(0)

            dve.wait_ge(edges_loaded[2], 16 * LOADS)
            dve.wait_ge(small_loaded, 16 * SMALL_DMAS)
            nc.vector.tensor_copy(dst_of[:, :, 1, :], dst_i[:, :, :]).then_inc(dst_step, 1)
            dve.wait_ge(dst_step, 1)
            nc.vector.tensor_tensor(dst_of[:, :, 0, :], dst_of[:, :, 1, :],
                                    base_f[:, :].unsqueeze(2).to_broadcast([P, GROUPS, TW]),
                                    ALU.subtract).then_inc(dst_step, 1)
            dve.wait_ge(dst_step, 2)

            dve.wait_ge(consts_made, 8)
            nc.vector.tensor_copy(iota_ps[:, 0:WIN], iota_f[:, 0:WIN]).then_inc(iota_placed, 1)
            inside = dst_of[:, :, 0, :]
            nc.vector.tensor_reduce(checks[:, 0:1], inside, AX.XY, ALU.max).then_inc(check_step, 1)
            nc.vector.tensor_reduce(checks[:, 1:2], inside, AX.XY, ALU.min).then_inc(check_step, 1)
            nc.vector.tensor_reduce(checks[:, 2:3], base_over[:, :], AX.X, ALU.min).then_inc(check_step, 1)
            dve.wait_ge(check_step, 4)
            nc.vector.tensor_scalar(checks[:, 3:4], checks[:, 0:1], float(WIN), None, ALU.is_ge).then_inc(check_step, 1)
            nc.vector.tensor_scalar(checks[:, 4:6], checks[:, 1:3], 0.0, None, ALU.is_lt).then_inc(check_step, 1)
            dve.wait_ge(check_step, 6)
            nc.vector.tensor_reduce(bad_edges[:, :], checks[:, 3:6], AX.X, ALU.add).then_inc(check_step, 1)
            dve.wait_ge(check_summed, 1)
            nc.vector.tensor_scalar(spread_ok[:, :], iota_ps[0:1, 256:257], 0.0, None, ALU.is_equal
                                    ).then_inc(check_step, 1)
            dve.wait_ge(check_step, 8)

            dve.wait_ge(edges_loaded[3], 16 * LOADS)
            for v in range(HALVES):
                stage_edges(0, 0, v)

            def gated_rows():
                dve.wait_ge(edges_loaded[4], 16 * LOADS)
                nc.vector.tensor_copy(row_of[1][:, :, :], type_i[1][:, :, :]).then_inc(gated_row_step, 1)
                dve.wait_ge(gated_row_step, 1)
                nc.vector.tensor_tensor(row_of[1][:, :, :], row_of[1][:, :, :], src_row[:, :, :],
                                        ALU.add).then_inc(gated_row_step, 1)
                dve.wait_ge(gated_row_step, 2)

            def read_y(layer, b, buf):
                m = norm_number(layer, b)
                if layer == GATED:
                    dve.wait_ge(relu_ready, m - BLOCKS + 1)
                    nc.vector.tensor_tensor(y_t[buf][:, :], relu_t[buf][:, :], residual[:, nodes(b)], ALU.add
                                            ).then_inc(y_ready, 1)
                else:
                    nc.vector.tensor_tensor(y_t[buf][:, :], sums[:, nodes(b)], residual[:, nodes(b)], ALU.add
                                            ).then_inc(y_ready, 1)

            def layernorm(layer, b, buf):
                m = norm_number(layer, b)
                dve.wait_ge(y_turned, m + 1)
                nc.vector.bn_stats(stats[buf][:, :], turns[buf][0:BLOCK, 0:D])
                dve.drain()
                nc.vector.bn_aggr(mean_var[buf][:, :], stats[buf][:, :]).then_inc(variance_ready, 1)
                dve.wait_ge(std_ready, m + 1)
                nc.vector.reciprocal(rstd[buf][:, :], std[buf][:, :]).then_inc(rstd_ready, 1)
                dve.wait_ge(rstd_ready, m + 1)
                if layer == GATED and not (isinstance(b, int) and out_uses(b, buf) == 0):
                    dve.wait_ge(out_stored[buf], 16 * out_uses(b, buf))
                nc.vector.tensor_scalar(norm[buf][:, :], turns[buf][0:BLOCK, 0:D], mean_var[buf][:, 0:1], rstd[buf][:, 0:1],
                                        ALU.subtract, ALU.mult).then_inc(norm_ready, 1)

            def gate_logits(layer, b, buf):
                m, n = norm_number(layer, b), block_number(layer, b)
                dve.wait_ge(multiplied, n + 1)
                nc.vector.tensor_tensor(logits[buf][:, :], product[0:BLOCK, 2 * buf + 1, D:D + R1],
                                        gate_b_all[0:BLOCK, :], ALU.add).then_inc(logits_ready, 1)
                nc.vector.tensor_copy(residual[:, nodes(b)], h_t[buf][:, 0:BLOCK]).then_inc(residual_kept, 1)

            def norm_blocks(layer, blocks):
                if layer < 2:
                    return
                for b, buf in blocks:
                    read_y(layer, b, buf)
                for b, buf in blocks:
                    layernorm(layer, b, buf)
                if layer == 2:
                    for b, buf in blocks:
                        gate_logits(layer, b, buf)

            def sorted_layer(layer):
                k0 = layer * GROUPS

                def onehots(k, v):
                    dve.wait_ge(edges_staged, k + 1)
                    for j in range(TW):
                        last = nc.vector.tensor_scalar(onehot[v][:, j, :], iota_ps[:, 0:WIN], dst_now[v][:, 0, j:j + 1],
                                                       weight_now[v][:, j:j + 1], ALU.is_equal, ALU.mult)
                    last.then_inc(onehots_ready, 1)

                def add_window(t, k, v):
                    start = dve.value_load(base_row[0:1, bass.ds(t * HALVES + v, 1)], min_val=0, max_val=N_NODES - 1)
                    dve.wait_ge(tiles_summed, (k - k0) * TW + (layer * ITERS * TI + TW))
                    dve.wait_ge(windows_added, k + 2)
                    at = sums[:, bass.ds(start, WIN)]
                    nc.vector.tensor_tensor(at, at, window[v][:, 0:WIN], ALU.add).then_inc(windows_added, 1)

                def add_norm(b, buf):
                    layernorm(layer, b, buf)
                    if layer == 2:
                        gate_logits(layer, b, buf)

                def iteration(t, b, last=False):
                    k = t * HALVES + k0
                    onehots(k + 1, 1)
                    if b is not None and layer >= 2:
                        if layer == 2:
                            dve.wait_ge(windows_added, k + 2)
                        read_y(layer, b, 0)
                    add_window(t, k, 0)
                    if not last:
                        stage(layer, t + 1, 0)
                        onehots(k + 2, 0)
                    if b is not None and layer >= 2:
                        add_norm(b, 0)
                    if last and layer >= 2:
                        if layer == 2:
                            dve.wait_ge(windows_added, k + 3)
                        norm_blocks(layer, ENDS[0:1])
                    add_window(t, k + 1, 1)
                    if not last:
                        stage(layer, t + 1, 1)

                if layer > 0:
                    stage(layer, 0, 0)
                    stage(layer, 0, 1)
                onehots(k0, 0)
                if layer > 0:
                    clear_sums(layer)
                with dve.Fori(0, LAG) as t:
                    iteration(t, None)
                if layer == 0:
                    gated_rows()
                iteration(LAG, 0)
                with dve.Fori(LAG + 1, ITERS - 1) as t:
                    iteration(t, t - LAG)
                iteration(ITERS - 1, ITERS - 1 - LAG, last=True)
                if layer == 2:
                    dve.wait_ge(windows_added, 2 + k0 + GROUPS)
                norm_blocks(layer, ENDS[1:])

            def unsorted_layer(layer):
                k0, n0 = layer * GROUPS, layer * ITERS * TI
                if layer == 0:
                    gated_rows()
                else:
                    clear_sums(layer)

                def stage_both(t):
                    for u in range(HALVES):
                        stage(layer, t, u)

                def sum_iteration(t):
                    for v in range(HALVES):
                        dve.wait_ge(edges_staged, (t + 1) * HALVES + k0)
                        for q in range(NCHUNK):
                            last = nc.vector.tensor_scalar(dst_shift[:, q, :], dst_now[v][:, 1, :], float(-q * CHUNK),
                                                           None, ALU.add)
                        last.then_inc(shifted, 1)
                        dve.wait_ge(shifted, t * HALVES + (k0 + v + 1))
                        for j in range(TW):
                            for q in range(NCHUNK):
                                m = t * (TI * NCHUNK) + ((n0 + v * TW + j) * NCHUNK + q)
                                nc.vector.tensor_scalar(wide_onehot[:, :], iota_f[:, :], dst_shift[:, q, j:j + 1],
                                                        weight_now[v][:, j:j + 1], ALU.is_equal, ALU.mult
                                                        ).then_inc(wide_ready, 1)
                                dve.wait_ge(wide_summed, m + 1)
                                at = sums[:, q * CHUNK:(q + 1) * CHUNK].rearrange("p (a b) -> p a b", a=4)
                                nc.vector.tensor_tensor(at, at, product[:, :, 0:CW], ALU.add).then_inc(wide_added, 1)

                if layer > 0:
                    stage_both(0)
                sum_iteration(0)
                with dve.Fori(1, ITERS) as t:
                    stage_both(t)
                    sum_iteration(t)
                dve.wait_ge(wide_added, (layer + 1) * ITERS * TI * NCHUNK)
                dve.sem_inc(windows_added, GROUPS)
                if layer >= 2:
                    norm_blocks(layer, [(0, 0)])
                    with dve.Fori(1, MAIN_BLOCKS) as b:
                        norm_blocks(layer, [(b, 0)])
                norm_blocks(layer, ENDS[0:1])
                norm_blocks(layer, ENDS[1:])

            flag = dve.value_load(spread_ok[0:1, 0:1], min_val=0, max_val=1)
            with dve.If(flag > 0):
                for layer in range(LAYERS):
                    sorted_layer(layer)
            with dve.Else():
                for layer in range(LAYERS):
                    unsorted_layer(layer)

        @block.tensor
        def _(pe):
            def turn_x(n, buf, x_buf, uses, rows=P):
                pe.wait_ge(x_loaded[x_buf], 16 * (uses + 1))
                nc.tensor.transpose(turns[buf][:, 0:rows], x_in[x_buf][0:rows, :],
                                    ident[0:rows, 0:rows]).then_inc(x_turned, 1)

            def multiply(layer, n, buf, rows=BLOCK):
                pe.wait_ge(h_ready, n + 1)
                w = weights[layer + 1]
                cols = GCOLS if layer + 1 == GATED else SLOTS_PER_NODE * D
                nc.tensor.matmul(product[0:rows, 2 * buf, :], h_t[buf][:, 0:rows], w[:, 0:512], start=True, stop=True)
                nc.tensor.matmul(product[0:rows, 2 * buf + 1, 0:cols - 512], h_t[buf][:, 0:rows], w[:, 512:cols],
                                 start=True, stop=True).then_inc(multiplied, 1)

            pe.wait_ge(consts_made, 3)
            turn_x(0, 0, 0, 0)
            turn_x(1, 1, 1, 0)
            pe.wait_ge(first_loaded, 16)

            def first_block(n, r, uses, peeled=False):
                rows = XLAST if isinstance(n, int) and n + 2 == XBLOCKS - 1 else P
                pe.wait_ge(residual_kept, n + 1)
                turn_x(n + 2, r % 2, (r + 2) % 4, uses, rows)
                if not peeled:
                    pe.wait_ge(rows_ready, n - 1)
                multiply(-1, n, r % 2, P)

            for r in range(4):
                first_block(r, r, r // 2, peeled=r < 2)
            with pe.Fori(1, XBLOCKS // 4 - 1) as q:
                for r in range(4):
                    first_block(4 * q + r, r, q + r // 2)
            for n in range(XBLOCKS - 5, XBLOCKS):
                if n + 2 < XBLOCKS:
                    first_block(n, n % 4, n // 4 + n % 4 // 2)
                else:
                    pe.wait_ge(rows_ready, n - 1)
                    multiply(-1, n, n % 2, XLAST if n == XBLOCKS - 1 else P)

            pe.wait_ge(check_step, 7)
            nc.tensor.matmul(iota_ps[0:1, 256:257], bad_edges[:, :], ones_col[:, :], start=True, stop=True
                             ).then_inc(check_summed, 1)

            def turn_y(layer, b, buf):
                m = norm_number(layer, b)
                pe.wait_ge(y_ready, m + 1)
                nc.tensor.transpose(turns[buf][0:BLOCK, 0:D], y_t[buf][:, :], ident[:, :]).then_inc(y_turned, 1)

            def turn_norm(layer, b, buf):
                m = norm_number(layer, b)
                pe.wait_ge(norm_ready, m + 1)
                nc.tensor.transpose(turns[buf][:, P:P + BLOCK], norm[buf][:, :], ident[0:BLOCK, 0:BLOCK]
                                    ).then_inc(norm_turned, 1)

            def multiply_block(layer, b, buf):
                n = block_number(layer, b)
                pe.wait_ge(rows_ready, n - 1 if isinstance(b, int) and b in TAIL else n)
                multiply(layer, n, buf)

            def turn_blocks(layer, blocks):
                if layer >= 2:
                    for b, buf in blocks:
                        turn_y(layer, b, buf)
                if layer == 2:
                    for b, buf in blocks:
                        turn_norm(layer, b, buf)
                if layer < GATED:
                    for b, buf in blocks:
                        multiply_block(layer, b, buf)

            def wait_weights():
                pe.wait_ge(weights_loaded, 16 * (LAYERS - 1))
                pe.wait_ge(small_loaded, 16 * SMALL_DMAS)

            def sorted_layer(layer):
                def tile(c, v, j):
                    s = v * TW + j
                    pe.wait_ge(landed[s], 16 * c + 16)
                    nc.tensor.matmul(window[v][:, 0:WIN], gathered[:, s, :], onehot[v][:, j, :],
                                     start=(j == 0), stop=(j == TW - 1)).then_inc(tiles_summed, 1)

                def iteration(t, b, last=False):
                    c = t + layer * ITERS
                    k = t * HALVES + layer * GROUPS
                    for v in range(HALVES):
                        pe.wait_ge(onehots_ready, k + v + 1)
                        pe.wait_ge(windows_added, k + v + 1)
                        for j in range(TW):
                            tile(c, v, j)
                            if b is None:
                                continue
                            if layer >= 2 and (v, j) == (0, 6):
                                turn_y(layer, b, 0)
                            if layer == 2 and (v, j) == (1, 2 if last else 4):
                                turn_norm(layer, b, 0)
                            if layer < GATED and (v, j) == (1, 4 if last else 8):
                                multiply_block(layer, b, 0)
                            if last and layer >= 2 and (v, j) == (1, 6):
                                turn_y(layer, *ENDS[0])
                            if last and layer == 2 and (v, j) == (1, 8):
                                turn_norm(layer, *ENDS[0])
                            if last and layer < GATED and (v, j) == (1, 10):
                                multiply_block(layer, *ENDS[0])

                with pe.Fori(0, LAG) as t:
                    iteration(t, None)
                if layer == 0:
                    wait_weights()
                with pe.Fori(LAG, ITERS - 1) as t:
                    iteration(t, t - LAG)
                iteration(ITERS - 1, ITERS - 1 - LAG, last=True)
                turn_blocks(layer, ENDS[1:])

            def unsorted_layer(layer):
                n0 = layer * ITERS * TI
                with pe.Fori(0, ITERS) as t:
                    for s in range(TI):
                        pe.wait_ge(landed[s], 16 * t + 16 * (layer * ITERS + 1))
                        for q in range(NCHUNK):
                            m = t * (TI * NCHUNK) + ((n0 + s) * NCHUNK + q)
                            pe.wait_ge(wide_ready, m + 1)
                            for a in range(4):
                                last = nc.tensor.matmul(product[:, a, 0:CW], gathered[:, s, :],
                                                        wide_onehot[:, a * CW:(a + 1) * CW], start=True, stop=True)
                            last.then_inc(wide_summed, 1)
                if layer == 0:
                    wait_weights()
                with pe.Fori(0, MAIN_BLOCKS) as b:
                    turn_blocks(layer, [(b, 0)])
                turn_blocks(layer, ENDS[0:1])
                turn_blocks(layer, ENDS[1:])

            pe.wait_ge(check_step, 8)
            flag = pe.value_load(spread_ok[0:1, 0:1], min_val=0, max_val=1)
            with pe.If(flag > 0):
                for layer in range(LAYERS):
                    sorted_layer(layer)
            with pe.Else():
                for layer in range(LAYERS):
                    unsorted_layer(layer)


_INS = ['x', 'src', 'dst', 'edge_type_5', 'edge_type_8', 'edge_weight1', 'L0_gnn_W_in', 'L0_gnn_W_hid',
        'L0_gnn_W_out', 'L1_gnn_weight', 'L1_gnn_gate_weight', 'L1_gnn_gate_bias', 'L1_gnn_bias']


def kernel(**inputs):
    import numpy as np
    import concourse.bacc as bacc
    from concourse.bass_utils import run_bass_kernel_spmd

    nc = bacc.Bacc("TRN2", target_bir_lowering=False, num_devices=1)
    arrays, args = {}, []
    for name in _INS:
        a = np.ascontiguousarray(inputs[name])
        arrays[f"in_{name}"] = a
        args.append(nc.dram_tensor(f"in_{name}", a.shape, mybir.dt.from_np(a.dtype), kind="ExternalInput").ap())
    args.append(nc.dram_tensor("out_0", (N_NODES, D), f32, kind="ExternalOutput").ap())
    gnn_program(nc, *args)
    r = run_bass_kernel_spmd(nc, [arrays], core_ids=[0])
    return r.results[0]["out_0"]
```
